# Optimizing a Trainium2 kernel written in Bass

```python
import numpy as np
import jax
import jax.numpy as jnp

def _softmax(x, axis=-1):
    return jax.nn.softmax(x, axis=axis)
def _gelu(x):
    return jax.nn.gelu(x, approximate=True)
def _silu(x):
    return jax.nn.silu(x)
def _sigmoid(x):
    return jax.nn.sigmoid(x)
def _layernorm(x, axis=-1, eps=1e-5):
    m = jnp.mean(x, axis=axis, keepdims=True)
    v = jnp.var(x, axis=axis, keepdims=True)
    return (x - m) / jnp.sqrt(v + eps)
def _scatter_add(tgt, idx, src, axis=0):
    return tgt.at[idx].add(src)
def _segment_sum(src, seg, n):
    return jax.ops.segment_sum(src, seg, n)

kernel_name = 'mk_conv_preact_d2_conv_nchw256_0340c3'

def setup_inputs(seed: int = 0):
    np.random.seed(seed)
    _w = jnp.asarray
    def _rec_inputs():
        import jax
        import jax.numpy as jnp
        _gk = jax.random.key(seed)
        x = -0.000125 + 0.9999 * jax.random.normal(jax.random.fold_in(_gk, 1), (8, 256, 128, 128), jnp.float32)
        return x
    x = _rec_inputs()
    def _L0_conv_setup():
        import jax, jax.numpy as jnp
        import numpy as np
        B, C, H, W = (8, 256, 128, 128)
        K = 3
        GC = 16
        G = C // GC
        RED = 4
        CR = C // RED
        PAD = (K - 1) // 2

        def _forward(x, w1, b1, wd, bd, w2, b2):
            y = jnp.einsum('oc,bchw->bohw', w1, x) + b1[None, :, None, None]
            y = jax.lax.conv_general_dilated(y, wd, window_strides=(1, 1), padding=[(PAD, PAD), (PAD, PAD)], feature_group_count=CR, dimension_numbers=('NCHW', 'OIHW', 'NCHW')) + bd[None, :, None, None]
            w = jnp.einsum('oc,bchw->bohw', w2, y) + b2[None, :, None, None]
            w = w.reshape(B, G, K, K, H, W)
            xr = x.reshape(B, G, GC, H, W)
            xp = jnp.pad(xr, ((0, 0), (0, 0), (0, 0), (PAD, PAD), (PAD, PAD)))
            out = jnp.zeros((B, G, GC, H, W), dtype=x.dtype)
            for kh in range(K):
                for kw in range(K):
                    out = out + xp[:, :, :, kh:kh + H, kw:kw + W] * w[:, :, kh, kw][:, :, None, :, :]
            return out.reshape(B, C, H, W)
        key = jax.random.key(seed)
        ks = jax.random.split(key, 8)
        s = 0.05
        return {'x': jax.random.normal(ks[0], (B, C, H, W), dtype=jnp.float32), 'w1': jax.random.normal(ks[1], (CR, C), dtype=jnp.float32) * s, 'b1': jax.random.normal(ks[2], (CR,), dtype=jnp.float32) * s, 'wd': jax.random.normal(ks[3], (CR, 1, K, K), dtype=jnp.float32) * s, 'bd': jax.random.normal(ks[4], (CR,), dtype=jnp.float32) * s, 'w2': jax.random.normal(ks[5], (K * K * G, CR), dtype=jnp.float32) * s, 'b2': jax.random.normal(ks[6], (K * K * G,), dtype=jnp.float32) * s}
    _L0_conv_all = _L0_conv_setup()
    _L0_conv_in = {k: v for k, v in _L0_conv_all.items() if k in ('w1', 'b1', 'wd', 'bd', 'w2', 'b2', )}
    del _L0_conv_all

    def _L1_conv_setup():
        import jax, jax.numpy as jnp
        import numpy as np
        B, C, H, W = (8, 256, 128, 128)
        NUM_HEADS = 8
        EPS = 1e-06
        key = jax.random.key(seed)
        ks = jax.random.split(key, 7)
        s = 1.0 / np.sqrt(C)
        return {'x': jax.random.normal(ks[0], (B, C, H, W), dtype=jnp.float32), 'Wq': jax.random.normal(ks[1], (C, C), dtype=jnp.float32) * s, 'bq': jax.random.normal(ks[2], (C,), dtype=jnp.float32) * 0.01, 'Wk': jax.random.normal(ks[3], (C, C), dtype=jnp.float32) * s, 'bk': jax.random.normal(ks[4], (C,), dtype=jnp.float32) * 0.01, 'Wv': jax.random.normal(ks[5], (C, C), dtype=jnp.float32) * s, 'bv': jax.random.normal(ks[6], (C,), dtype=jnp.float32) * 0.01}
    _L1_conv_all = _L1_conv_setup()
    _L1_conv_in = {k: v for k, v in _L1_conv_all.items() if k in ('Wq', 'bq', 'Wk', 'bk', 'Wv', 'bv', )}
    del _L1_conv_all

    return {
        "x": x,
        "L0_conv_w1": _L0_conv_in["w1"],
        "L0_conv_b1": _L0_conv_in["b1"],
        "L0_conv_wd": _L0_conv_in["wd"],
        "L0_conv_bd": _L0_conv_in["bd"],
        "L0_conv_w2": _L0_conv_in["w2"],
        "L0_conv_b2": _L0_conv_in["b2"],
        "L1_conv_Wq": _L1_conv_in["Wq"],
        "L1_conv_bq": _L1_conv_in["bq"],
        "L1_conv_Wk": _L1_conv_in["Wk"],
        "L1_conv_bk": _L1_conv_in["bk"],
        "L1_conv_Wv": _L1_conv_in["Wv"],
        "L1_conv_bv": _L1_conv_in["bv"],
    }

def reference(x, L0_conv_w1, L0_conv_b1, L0_conv_wd, L0_conv_bd, L0_conv_w2, L0_conv_b2, L1_conv_Wq, L1_conv_bq, L1_conv_Wk, L1_conv_bk, L1_conv_Wv, L1_conv_bv):
    import jax
    import jax.numpy as jnp
    def _L0_conv_ref(x, w1, b1, wd, bd, w2, b2):
        import jax, jax.numpy as jnp
        import numpy as np
        B, C, H, W = (8, 256, 128, 128)
        K = 3
        GC = 16
        G = C // GC
        RED = 4
        CR = C // RED
        PAD = (K - 1) // 2

        def _forward(x, w1, b1, wd, bd, w2, b2):
            y = jnp.einsum('oc,bchw->bohw', w1, x) + b1[None, :, None, None]
            y = jax.lax.conv_general_dilated(y, wd, window_strides=(1, 1), padding=[(PAD, PAD), (PAD, PAD)], feature_group_count=CR, dimension_numbers=('NCHW', 'OIHW', 'NCHW')) + bd[None, :, None, None]
            w = jnp.einsum('oc,bchw->bohw', w2, y) + b2[None, :, None, None]
            w = w.reshape(B, G, K, K, H, W)
            xr = x.reshape(B, G, GC, H, W)
            xp = jnp.pad(xr, ((0, 0), (0, 0), (0, 0), (PAD, PAD), (PAD, PAD)))
            out = jnp.zeros((B, G, GC, H, W), dtype=x.dtype)
            for kh in range(K):
                for kw in range(K):
                    out = out + xp[:, :, :, kh:kh + H, kw:kw + W] * w[:, :, kh, kw][:, :, None, :, :]
            return out.reshape(B, C, H, W)
        return _forward(x, w1, b1, wd, bd, w2, b2)

    def _L1_conv_ref(x, Wq, bq, Wk, bk, Wv, bv):
        import jax, jax.numpy as jnp
        import numpy as np
        B, C, H, W = (8, 256, 128, 128)
        NUM_HEADS = 8
        EPS = 1e-06
        b, c_full, h_sp, w_sp = x.shape
        p = NUM_HEADS
        c = c_full // p
        n = h_sp * w_sp

        def proj(Wm, bm):
            return jnp.einsum('bchw,oc->bohw', x, Wm) + bm[None, :, None, None]
        q = jax.nn.softplus(proj(Wq, bq)).reshape(b, p, c, n).transpose(0, 1, 3, 2)
        k = jax.nn.softplus(proj(Wk, bk)).reshape(b, p, c, n)
        v = proj(Wv, bv).reshape(b, p, c, n)
        kv = jnp.einsum('bpmn,bpcn->bpmc', k, v)
        norm = 1.0 / jnp.einsum('bpnc,bpc->bpn', q, jnp.sum(k, axis=-1) + EPS)
        out = jnp.einsum('bpnm,bpmc,bpn->bpcn', q, kv, norm)
        return out.reshape(b, c_full, h_sp, w_sp)

    def _gn(v, G=32, eps=1e-5):
        B_, C_, H_, W_ = v.shape
        g = v.reshape(B_, G, C_ // G, H_, W_)
        m = jnp.mean(g, axis=(2, 3, 4), keepdims=True)
        s = jnp.var(g, axis=(2, 3, 4), keepdims=True)
        return ((g - m) / jnp.sqrt(s + eps)).reshape(v.shape)

    def _ln_c(v, eps=1e-6):
        m = jnp.mean(v, axis=1, keepdims=True)
        s = jnp.var(v, axis=1, keepdims=True)
        return (v - m) / jnp.sqrt(s + eps)

    def _ln_t(v, eps=1e-5):
        m = jnp.mean(v, axis=-1, keepdims=True)
        s = jnp.var(v, axis=-1, keepdims=True)
        return (v - m) / jnp.sqrt(s + eps)

    def _to_tokens(v):
        B_, C_, H_, W_ = v.shape
        return v.reshape(B_, C_, H_ * W_).transpose(0, 2, 1)
    def _from_tokens(t, like):
        B_, C_, H_, W_ = like.shape
        return t.transpose(0, 2, 1).reshape(B_, C_, H_, W_)

    x = x + _L0_conv_ref(_gn(x), L0_conv_w1, L0_conv_b1, L0_conv_wd, L0_conv_bd, L0_conv_w2, L0_conv_b2)
    x = x + _L1_conv_ref(_gn(x), L1_conv_Wq, L1_conv_bq, L1_conv_Wk, L1_conv_bk, L1_conv_Wv, L1_conv_bv)
    return x


_drawn_inputs = setup_inputs


def setup_inputs(seed=0):
    import zlib

    import numpy as np

    out = dict(_drawn_inputs(seed))
    spreads = {}
    factors = {'L0_conv_b1': 8.0,
     'L1_conv_Wq': 8.0,
     'L1_conv_bq': 200.0,
     'L1_conv_Wk': 7.461,
     'L1_conv_bk': 200.0,
     'L1_conv_Wv': 5.066,
     'L1_conv_bv': 5.645}
    for name, (base, spread) in spreads.items():
        noise = np.random.default_rng([zlib.crc32(name.encode()), seed]).standard_normal(out[name].shape)
        drawn = base * np.exp(spread * noise) if base else spread * noise
        out[name] = jnp.asarray(drawn.astype(out[name].dtype))
    for name, factor in factors.items():
        out[name] = (out[name] * factor).astype(out[name].dtype)
    return out
```

```python
from contextlib import ExitStack

import concourse.bass as bass
from concourse import mybir

F32 = mybir.dt.float32
BF16 = mybir.dt.bfloat16
ALU = mybir.AluOpType
ACT = mybir.ActivationFunctionType

P = 128
IMAGES, CH, ROWS, COLS = 8, 256, 128, 128
HALVES = CH // P
PIX = ROWS * COLS
TAPS = 9
KW = 3
GROUPS = 16
GC = CH // GROUPS
CR = 64
NW = TAPS * GROUPS
BR = 4
NB = ROWS // BR
BP = BR * COLS
PADW = COLS + 2
RING = 8
ROWT = KW * CH
FILLS = BR * KW * HALVES // 4
PAIRS = ROWS // 2
HEADS = 8
GN_EPS = 1e-5
KSUM_EPS = 1e-6
BIAS_ROWS = 96
DEN_COLS = 32


def two_block_kernel(nc, x, w1t, b1, wd, bd, w2t, b2, wqkv, bqkv, ident_in, gmean_in, headmask_in, densel_in, headsel_in, out):
    x_v = x.rearrange("b (h p) r c -> b p h (r c)", p=P)
    out_v = out.rearrange("b (h p) r c -> b p h (r c)", p=P)

    with ExitStack() as ctx:
        def sb(name, shape, dt=F32):
            return ctx.enter_context(nc.sbuf_tensor(name, shape, dt))

        def sem(name):
            return ctx.enter_context(nc.semaphore(name))

        X = sb("X", [P, HALVES, PIX])
        w1_s = sb("w1_s", [P, HALVES, P])
        b1_s = sb("b1_s", [P, 1])
        wd_s = sb("wd_s", [P, TAPS])
        wdiag = sb("wdiag", [P, TAPS, P])
        zero_row = sb("zero_row", [P, PADW])
        bd_s = sb("bd_s", [P, 1])
        w2_s = sb("w2_s", [P, NW])
        w_gn = sb("w_gn", [P, HALVES, 3 * CH])
        bqkv_row = sb("bqkv_row", [1, 3 * CH])
        ident = sb("ident", [P, P])
        gmean = sb("gmean", [P, P])
        headmask = sb("headmask", [P, P])
        densel = sb("densel", [P, HALVES, DEN_COLS])
        ones_bf = sb("ones_bf", [BIAS_ROWS, BP], BF16)
        b2_parts = sb("b2_parts", [BIAS_ROWS, NW], BF16)
        qk_parts = sb("qk_parts", [BIAS_ROWS, 2 * CH], BF16)

        stats = sb("stats", [P, HALVES, NB, 6])
        mean_var = sb("mean_var", [P, HALVES, 2])
        gn_mean = sb("gn_mean", [P, 2])
        gn_avg = sb("gn_avg", [P, 2])
        gn_dev = sb("gn_dev", [P, 2])
        gn_var = sb("gn_var", [P, 2])
        gn_ln = sb("gn_ln", [P, 2])
        gn_r0 = sb("gn_r0", [P, 2])
        gn_t = sb("gn_t", [P, 2])
        gn_rstd = sb("gn_rstd", [P, 2])
        gn_shift = sb("gn_shift", [P, 2])
        gn_neg = sb("gn_neg", [P, 2])

        xn = sb("xn", [P, 2, HALVES, BR, PADW])
        y = sb("y", [P, 2, BR, PADW])
        y_last = sb("y_last", [CR, COLS])
        y2 = sb("y2", [P, 2, 2, COLS])
        sums = w_gn[:, :, :].rearrange("p h m -> p (h m)").rearrange("p (s k c) -> p s k c", s=2, k=KW)
        arena = sb("arena", [P, RING * ROWT + 2 * TAPS * CH])
        xt = arena[:, 0:RING * ROWT]
        prod = arena[:, RING * ROWT:].rearrange("p (s k c) -> p s k c", s=2, k=TAPS)

        at = [0]

        def piece(n):
            at[0] += n
            return arena[:, at[0] - n:at[0]]

        xs = piece(2 * HALVES * 2 * P).rearrange("p (s h n) -> p s h n", s=2, h=HALVES)
        k_act = piece(2 * 2 * CH).rearrange("p (s n) -> p s n", s=2)
        k_sb = piece(2 * 2 * CH).rearrange("p (s t m) -> p s t m", s=2, t=2)
        XO = CH + 1
        xt_sb = piece(2 * 2 * XO).rearrange("p (s t m) -> p s t m", s=2, t=2)
        kx_sb = piece(HALVES * XO).rearrange("p (h m) -> p h m", h=HALVES)
        kxt_sb = piece(HALVES * CH).rearrange("p (h m) -> p h m", h=HALVES)
        bias_row = piece(3 * CH)[0:1, :]
        ksum_row = piece(CH)[0:1, :]
        b2_row = piece(NW)[0:1, :]
        part_rest = piece(2 * CH)[0:1, :]
        part_mid = piece(2 * CH)[0:1, :].bitcast(BF16)[:, 0:2 * CH]
        kv_w = piece(HALVES * P).rearrange("p (h n) -> p h n", h=HALVES)
        den_w = piece(HALVES * DEN_COLS).rearrange("p (h n) -> p h n", h=HALVES)
        fold_start = at[0] - HALVES * (P + DEN_COLS)
        headsel = piece(BR * HALVES * P).rearrange("p (c h n) -> p c h n", c=BR, h=HALVES)
        assert at[0] <= RING * ROWT + 2 * TAPS * CH
        at[0] = 0
        q_act = piece(2 * HALVES * BP).rearrange("p (s h n) -> p s h n", s=2, h=HALVES)
        q_sb = piece(2 * HALVES * BP).rearrange("p (s h n) -> p s h n", s=2, h=HALVES)
        rden_wide = piece(HALVES * BP).rearrange("p (h n) -> p h n", h=HALVES)
        ratio = piece(HALVES * BP).rearrange("p (h n) -> p h n", h=HALVES)
        rden = piece(P)
        assert at[0] <= fold_start

        ksum_eps = sb("ksum_eps", [P, HALVES])

        ps = ctx.enter_context(nc.psum_tensor("ps", [P, 8, 512], F32))
        XT_BANK, W_BANK, INV_BANK = 0, 4, 6
        Y_BANK, Y2_BANK = 2, 3
        KZ_BANK, KT_BANK, KX_BANK = 0, 2, 4
        QZ_BANK, NUM_BANK, DEN_BANK, WIDE_BANK = 0, 4, 6, (7, 6)
        GN_BANK, ROW_BANK = 2, 3

        const_loaded = sem("const_loaded")
        sel_loaded = sem("sel_loaded")
        w_loaded = sem("w_loaded")
        x_loaded = [sem("x_loaded0"), sem("x_loaded1")]
        out_stored = [sem("out_stored0"), sem("out_stored1")]
        init_done = sem("init_done")
        gn_in = sem("gn_in")
        gn_mm = sem("gn_mm")
        gn_root = sem("gn_root")
        gn_ready = sem("gn_ready")
        xn_ready = sem("xn_ready")
        y_mm = sem("y_mm")
        y_halo = sem("y_halo")
        y_evac = sem("y_evac")
        y2_mm = sem("y2_mm")
        y2_evac = sem("y2_evac")
        xt_mm = sem("xt_mm")
        xt_evac = sem("xt_evac")
        w_ready = sem("w_ready")
        mult_two = sem("mult_two")
        mult_done = sem("mult_done")
        sum_two = sem("sum_two")
        sum_done = sem("sum_done")
        inv_ready = sem("inv_ready")
        x1_done = sem("x1_done")
        w_scaled = sem("w_scaled")
        row_mm = sem("row_mm")
        bias_ready = sem("bias_ready")
        xs_ready = sem("xs_ready")
        kz_mm = sem("kz_mm")
        kt_mm = sem("kt_mm")
        kl_ready = sem("kl_ready")
        kt_evac = sem("kt_evac")
        k_ready = sem("k_ready")
        kx_done = sem("kx_done")
        fold_in = sem("fold_in")
        fold_mm = sem("fold_mm")
        qz_mm = sem("qz_mm")
        ql_ready = sem("ql_ready")
        q_ready = sem("q_ready")
        den_mm = sem("den_mm")
        rden_ready = sem("rden_ready")
        num_mm = sem("num_mm")
        wide_mm = sem("wide_mm")
        wide_evac = sem("wide_evac")
        num_read = sem("num_read")
        out_ready = sem("out_ready")

        N_CONST = 11
        block = ctx.enter_context(nc.Block())

        def images(eng, image):
            with eng.Fori(0, IMAGES - 1) as i:
                image(i, False)
            image(IMAGES - 1, True)

        def block_steps(eng, step):
            for s in range(-2, 2):
                step(s, s % 2)
            with eng.Fori(1, NB // 2 - 2) as j:
                step(2 * j, 0)
                step(2 * j + 1, 1)
            for s in range(NB - 4, NB):
                step(s, s % 2)

        def ahead(s, n):
            return not isinstance(s, int) or 0 <= s + n < NB

        def first(s, n):
            return isinstance(s, int) and s < n

        @block.sync
        def _(sp):
            for dst, src in ((w1_s[:, :, :], w1t.rearrange("(h p) n -> p h n", p=P)), (b1_s[:, :], b1), (wd_s[:, :], wd),
                             (bd_s[:, :], bd), (w2_s[:, :], w2t), (b2_row[:, :], b2),
                             (bqkv_row[:, :], bqkv),
                             (ident[:, :], ident_in), (gmean[:, :], gmean_in), (headmask[:, :], headmask_in),
                             (densel[:, :, :], densel_in)):
                sp.dma_start(dst, src).then_inc(const_loaded, 16)

            def load(i, t, par):
                sp.dma_start(X[:, :, bass.ds(t * BP, BP)], x_v[i, :, :, bass.ds(t * BP, BP)]).then_inc(x_loaded[par], 16)

            load(0, 0, 0)
            load(0, 1, 1)
            with sp.Fori(1, NB // 2) as j:
                sp.wait_ge(x_loaded[0], 16 * j)
                load(0, 2 * j, 0)
                sp.wait_ge(x_loaded[1], 16 * j)
                load(0, 2 * j + 1, 1)

            def image(i, last):
                def store(t, par):
                    sp.wait_ge(out_ready, NB * i + t + 1)
                    sp.dma_start(out_v[i, :, :, bass.ds(t * BP, BP)], X[:, :, bass.ds(t * BP, BP)]).then_inc(out_stored[par], 16)

                def next_load(t_half, par):
                    if not last:
                        sp.wait_ge(out_stored[par], 16 * (NB // 2 * i + t_half + 1))
                        sp.wait_ge(x_loaded[par], 16 * (NB // 2 * (i + 1) + t_half))
                        load(i + 1, 2 * t_half + par, par)

                sp.wait_ge(x1_done, PAIRS * (i + 1))
                sp.dma_start(w_gn[:, :, :], wqkv.rearrange("(h p) n -> p h n", p=P)).then_inc(w_loaded, 16)
                sp.wait_ge(gn_ready, 2 * i + 2)
                sp.dma_start(headsel, headsel_in).then_inc(sel_loaded, 16)
                store(0, 0)
                store(1, 1)
                next_load(0, 0)
                with sp.Fori(1, NB // 2) as j:
                    store(2 * j, 0)
                    next_load(j - 1, 1)
                    store(2 * j + 1, 1)
                    next_load(j, 0)
                next_load(NB // 2 - 1, 1)

            images(sp, image)
            for par in range(2):
                sp.wait_ge(out_stored[par], 16 * (NB // 2) * IMAGES)

        @block.gpsimd
        def _(pool):
            def image(i, last):
                def add_products(s, r):
                    row = BR * s + r
                    pool.wait_ge(mult_two, ROWS * i + row + 1)
                    if not (first(s, 1) and r < 2):
                        pool.wait_ge(inv_ready, ROWS * i + row - 1)
                    nc.gpsimd.tensor_tensor(sums[:, r % 2, :, :], prod[:, r % 2, 0:KW, :], prod[:, r % 2, KW:2 * KW, :],
                                            ALU.add).then_inc(sum_two, 1)
                    pool.wait_ge(mult_done, ROWS * i + row + 1)
                    pool.wait_ge(sum_two, ROWS * i + row + 1)
                    nc.gpsimd.tensor_tensor(sums[:, r % 2, :, :], sums[:, r % 2, :, :], prod[:, r % 2, 2 * KW:3 * KW, :],
                                            ALU.add).then_inc(sum_done, 1)

                for r in range(BR):
                    add_products(0, r)
                with pool.Fori(1, NB) as s:
                    for r in range(BR):
                        add_products(s, r)

            images(pool, image)

        @block.scalar
        def _(act):
            def gn_guess(n):
                act.wait_ge(gn_in, 3 * n + 3)
                nc.scalar.activation(gn_ln[:, :], gn_var[:, :], ACT.Ln)
                act.drain()
                nc.scalar.activation(gn_r0[:, :], gn_ln[:, :], ACT.Exp, scale=-0.5).then_inc(gn_root, 1)

            def normalise(i, b, par):
                if not first(b, 2):
                    act.wait_ge(xt_mm, FILLS * (NB * i + b - 1))
                for h in range(HALVES):
                    ins = nc.scalar.activation(
                        xn[:, par, h, :, 1:1 + COLS], X[:, h, bass.ds(b * BP, BP)].rearrange("p (r c) -> p r c", r=BR),
                        ACT.Identity, bias=gn_shift[:, h:h + 1], scale=gn_rstd[:, h:h + 1])
                ins.then_inc(xn_ready, 1)

            def y_out(i, b, par):
                act.wait_ge(y_mm, NB * i + b + 1)
                yp = ps[:, Y_BANK, :].rearrange("p (r c) -> p r c", r=BR)

                def put(lo, dst, src):
                    return nc.scalar.activation(dst, src, ACT.Identity, bias=b1_s[lo:lo + CR, :])

                if first(b, 1):
                    nc.scalar.copy(y[0:CR, par, 0, :], zero_row[0:CR, :])
                else:
                    put(CR, y[CR:P, 1 - par, BR - 1:BR, 1:1 + COLS], yp[CR:P, 0:1, :]).then_inc(y_halo, 1)
                    nc.scalar.copy(y[0:CR, par, 0, 1:1 + COLS], y_last[:, :])
                put(0, y[0:CR, par, 1:BR, 1:1 + COLS], yp[0:CR, 0:BR - 1, :])
                put(CR, y[CR:P, par, 0:BR - 1, 1:1 + COLS], yp[CR:P, 1:BR, :])
                if not (isinstance(b, int) and b == 0):
                    act.drain()
                put(0, y_last[:, :], yp[0:CR, BR - 1, :]).then_inc(y_evac, 1)
                if isinstance(b, int) and b == NB - 1:
                    nc.scalar.copy(y[CR:P, par, BR - 1, :], zero_row[CR:P, :]).then_inc(y_halo, 1)

            def y2_out(i, b, par):
                act.wait_ge(y2_mm, NB * i + b + 1)
                nc.scalar.activation(y2[:, par, :, :], ps[:, Y2_BANK, 0:2 * COLS].rearrange("p (r c) -> p r c", r=2),
                                     ACT.Identity, bias=bd_s[:, :]).then_inc(y2_evac, 1)

            def xt_out(i, b, par):
                if not first(b, 1):
                    act.wait_ge(mult_done, ROWS * i + BR * b - 3)
                for f in range(FILLS):
                    act.wait_ge(xt_mm, FILLS * (NB * i + b) + f + 1)
                    o = par * BR * ROWT + f * 512
                    nc.scalar.copy(xt[:, o:o + 512], ps[:, XT_BANK + f % 2, :]).then_inc(xt_evac, 1)

            def softplus_log(dst, z):
                nc.scalar.activation(dst, z, ACT.Abs)
                act.drain()
                nc.scalar.activation(dst, dst, ACT.Exp, scale=-1.0)
                act.drain()
                return nc.scalar.activation(dst, dst, ACT.Ln, bias=1.0)

            nc.scalar.preload_act_table_set("natural_log_exp_and_others")
            act.wait_ge(init_done, 1)
            gn_guess(0)

            def image(i, last):
                act.wait_ge(gn_ready, 2 * i + 1)
                normalise(i, 0, 0)

                def step(s, par):
                    if ahead(s, 2):
                        y_out(i, s + 2, par)
                    if ahead(s, 1):
                        xt_out(i, s + 1, 1 - par)
                        y2_out(i, s + 1, 1 - par)
                    if ahead(s, 3):
                        normalise(i, s + 3, 1 - par)

                block_steps(act, step)
                gn_guess(2 * i + 1)

                def k_pair(u, par):
                    act.wait_ge(kz_mm, PAIRS * i + u + 1)
                    if not first(u, 2):
                        act.wait_ge(k_ready, PAIRS * i + u - 1)
                    softplus_log(k_act[:, par, :], ps[:, KZ_BANK + par, :]).then_inc(kl_ready, 1)
                    act.wait_ge(kt_mm, PAIRS * i + u + 1)
                    if not first(u, 2):
                        act.wait_ge(kx_done, PAIRS * i + u - 1)
                    nc.scalar.copy(xt_sb[:, par, :, 0:CH], ps[:, KT_BANK + par, :].rearrange("p (t m) -> p t m", t=2)
                                   ).then_inc(kt_evac, 1)

                k_pair(0, 0)
                k_pair(1, 1)
                with act.Fori(1, PAIRS // 2) as j:
                    k_pair(2 * j, 0)
                    k_pair(2 * j + 1, 1)

                def q_log(t, par):
                    for h in range(HALVES):
                        act.wait_ge(qz_mm, 2 * (NB * i + t) + h + 1)
                        softplus_log(q_act[:, par, h, :], ps[:, QZ_BANK + 2 * par + h, :]).then_inc(ql_ready, 1)

                def wide_out(t):
                    for h in range(HALVES):
                        act.wait_ge(wide_mm, 2 * (NB * i + t) + h + 1)
                        if h == 0 and not first(t, 1):
                            act.wait_ge(num_read, NB * i + t)
                        nc.scalar.copy(rden_wide[:, h, :], ps[:, WIDE_BANK[h], :]).then_inc(wide_evac, 1)

                q_log(0, 0)
                q_log(1, 1)
                wide_out(0)
                with act.Fori(1, NB // 2) as j:
                    q_log(2 * j, 0)
                    wide_out(2 * j - 1)
                    q_log(2 * j + 1, 1)
                    wide_out(2 * j)
                wide_out(NB - 1)
                if not last:
                    gn_guess(2 * i + 2)

            images(act, image)

        @block.vector
        def _(dve):
            def stat(t):
                for h in range(HALVES):
                    nc.vector.bn_stats(stats[:, h, bass.ds(t, 1), :], X[:, h, bass.ds(t * BP, BP)])

            def stat_loaded(n, t, t_half, par):
                dve.wait_ge(x_loaded[par], 16 * (NB // 2 * n + t_half + 1))
                stat(t)

            def groupnorm(n):
                dve.drain()
                for h in range(HALVES):
                    ins = nc.vector.bn_aggr(mean_var[:, h, :], stats[:, h, :, :].rearrange("p t s -> p (t s)"))
                ins.then_inc(gn_in, 1)
                dve.wait_ge(gn_mm, 2 * n + 1)
                means = ps[:, GN_BANK, 0:4].rearrange("p (h s) -> p h s", h=2)
                nc.vector.tensor_copy(gn_mean[:, :], means[:, :, 0])
                nc.vector.tensor_copy(gn_avg[:, :], means[:, :, 1])
                dve.drain()
                nc.vector.tensor_tensor(gn_dev[:, :], mean_var[:, :, 0], gn_mean[:, :], ALU.subtract)
                dve.drain()
                nc.vector.tensor_tensor(gn_dev[:, :], gn_dev[:, :], gn_dev[:, :], ALU.mult).then_inc(gn_in, 1)
                dve.wait_ge(gn_mm, 2 * n + 2)
                nc.vector.scalar_tensor_tensor(gn_var[:, :], ps[:, GN_BANK, 4:6], GN_EPS, gn_avg[:, :],
                                               ALU.add, ALU.add).then_inc(gn_in, 1)
                dve.wait_ge(gn_root, n + 1)
                nc.vector.tensor_tensor(gn_t[:, :], gn_r0[:, :], gn_r0[:, :], ALU.mult)
                dve.drain()
                nc.vector.tensor_tensor(gn_t[:, :], gn_t[:, :], gn_var[:, :], ALU.mult)
                dve.drain()
                nc.vector.tensor_scalar(gn_t[:, :], gn_t[:, :], -0.5, 1.5, ALU.mult, ALU.add)
                dve.drain()
                nc.vector.tensor_tensor(gn_rstd[:, :], gn_r0[:, :], gn_t[:, :], ALU.mult)
                dve.drain()
                nc.vector.tensor_scalar(gn_neg[:, :], gn_mean[:, :], -1.0, None, ALU.mult)
                nc.vector.scalar_tensor_tensor(gn_shift[:, :], gn_mean[:, :], -1.0, gn_rstd[:, :],
                                               ALU.mult, ALU.mult).then_inc(gn_ready, 1)

            def in_parts(parts, row, n):
                dve.drain()
                nc.vector.tensor_copy(parts[0:1, 0:n], row)
                dve.drain()
                nc.vector.tensor_tensor(part_rest[:, 0:n], row, parts[0:1, 0:n], ALU.subtract)
                dve.drain()
                nc.vector.tensor_copy(part_mid[:, 0:n], part_rest[:, 0:n])
                dve.drain()
                nc.vector.tensor_copy(parts[32:33, 0:n], part_mid[:, 0:n])
                nc.vector.tensor_tensor(part_rest[:, 0:n], part_rest[:, 0:n], part_mid[:, 0:n], ALU.subtract)
                dve.drain()
                return nc.vector.tensor_copy(parts[64:65, 0:n], part_rest[:, 0:n])

            nc.vector.memset(xn[:, :, :, :, :], 0.0)
            nc.vector.memset(y[:, :, :, :], 0.0)
            nc.vector.memset(b2_parts[:, :], 0.0)
            nc.vector.memset(qk_parts[:, :], 0.0)
            nc.vector.memset(ones_bf[:, :], 1.0)
            nc.vector.memset(zero_row[:, :], 0.0)
            dve.wait_ge(const_loaded, 16 * N_CONST)
            for k in range(TAPS):
                nc.vector.tensor_scalar(wdiag[:, k, :], ident[:, :], wd_s[:, k:k + 1], None, ALU.mult)
            in_parts(b2_parts, b2_row[:, :], NW).then_inc(init_done, 1)
            with dve.Fori(0, NB // 2) as j:
                stat_loaded(0, 2 * j, j, 0)
                stat_loaded(0, 2 * j + 1, j, 1)
            groupnorm(0)

            def image(i, last):
                def products(s, par, r):
                    row = BR * s + r
                    dve.wait_ge(w_ready, ROWS * i + row + 1)
                    if not (first(s, 1) and r < 2):
                        dve.wait_ge(sum_done, ROWS * i + row - 1)
                    for kh in range(KW):
                        if kh == 2 and not (isinstance(s, int) and s == NB - 1 and r == BR - 1):
                            fills = (3, 5, 6, FILLS + 2)[r]
                            dve.wait_ge(xt_evac, FILLS * (NB * i + s) + fills)
                        slot = (BR * par + r + kh - 1) % RING
                        ins = nc.vector.tensor_tensor(
                            prod[:, r % 2, KW * kh:KW * kh + KW, :].rearrange("p k (g c) -> p (k g) c", c=GC),
                            ps[:, W_BANK + r % 2, 48 * kh:48 * kh + 48].unsqueeze(2).to_broadcast([P, 48, GC]),
                            xt[:, slot * ROWT:(slot + 1) * ROWT].rearrange("p (a c) -> p a c", c=GC), ALU.mult)
                        if kh == 1:
                            ins.then_inc(mult_two, 1)
                    ins.then_inc(mult_done, 1)

                def add_rows(s, pair):
                    q = 2 * s + pair
                    dve.wait_ge(inv_ready, ROWS * i + 2 * q + 2)
                    xa = X[:, :, bass.ds(q * 2 * COLS, 2 * COLS)]
                    nc.vector.tensor_tensor(xa, ps[:, INV_BANK + pair, :].rearrange("p (h n) -> p h n", h=2), xa,
                                            ALU.add).then_inc(x1_done, 1)

                def step(s, par):
                    if not ahead(s, 0):
                        return
                    products(s, par, 0)
                    products(s, par, 1)
                    if not first(s, 1):
                        add_rows(s - 1, 1)
                    products(s, par, 2)
                    if not first(s, 1):
                        dve.drain()
                        stat(s - 1)
                    if isinstance(s, int) and s == NB - 1:
                        nc.vector.memset(xt[:, 0:ROWT], 0.0)
                        dve.drain()
                    products(s, par, 3)
                    add_rows(s, 0)

                nc.vector.memset(xt[:, (RING - 1) * ROWT:RING * ROWT], 0.0)
                dve.drain()
                block_steps(dve, step)
                add_rows(NB - 1, 1)
                dve.drain()
                stat(NB - 1)
                groupnorm(2 * i + 1)

                dve.wait_ge(w_loaded, 16 * (i + 1))
                for h in range(HALVES):
                    ins = nc.vector.tensor_scalar(w_gn[:, h, :], w_gn[:, h, :], gn_rstd[:, h:h + 1], None, ALU.mult)
                ins.then_inc(w_scaled, 1)
                dve.wait_ge(row_mm, i + 1)
                nc.vector.tensor_tensor(bias_row[:, 0:2 * CH], ps[0:1, ROW_BANK, :], bqkv_row[:, 0:2 * CH], ALU.add)
                nc.vector.tensor_tensor(bias_row[:, 2 * CH:], ps[0:1, ROW_BANK + 1, 0:CH], bqkv_row[:, 2 * CH:], ALU.add)
                in_parts(qk_parts, bias_row[:, 0:2 * CH], 2 * CH).then_inc(bias_ready, 1)

                nc.vector.memset(xt_sb[:, :, :, CH:XO], 1.0)

                def copy_x(u, par):
                    if not first(u, 2):
                        dve.wait_ge(kt_mm, PAIRS * i + u - 1)
                    nc.vector.tensor_copy(xs[:, par, :, :], X[:, :, bass.ds(u * 2 * COLS, 2 * COLS)]).then_inc(xs_ready, 1)

                def k_sum(u, par):
                    dve.wait_ge(kl_ready, PAIRS * i + u + 1)
                    if not first(u, 2):
                        dve.wait_ge(kx_done, PAIRS * i + u - 1)
                    nc.vector.scalar_tensor_tensor(k_sb[:, par, :, :].rearrange("p t m -> p (t m)"), ps[:, KZ_BANK + par, :],
                                                   0.0, k_act[:, par, :], ALU.max, ALU.add).then_inc(k_ready, 1)

                copy_x(0, 0)
                copy_x(1, 1)
                k_sum(0, 0)
                with dve.Fori(1, PAIRS // 2) as j:
                    copy_x(2 * j, 0)
                    k_sum(2 * j - 1, 1)
                    copy_x(2 * j + 1, 1)
                    k_sum(2 * j, 0)
                k_sum(PAIRS - 1, 1)

                dve.wait_ge(kx_done, PAIRS * (i + 1))
                for h in range(HALVES):
                    ins = nc.vector.tensor_copy(kx_sb[:, h, :], ps[:, KX_BANK + h, 0:XO])
                ins.then_inc(fold_in, 1)
                dve.drain()
                nc.vector.tensor_scalar(ksum_eps[:, :], kx_sb[:, :, CH], KSUM_EPS, None, ALU.add)
                dve.drain()
                for h in range(HALVES):
                    nc.vector.tensor_scalar(den_w[:, h, :], densel[:, h, :], ksum_eps[:, h:h + 1], None, ALU.mult)
                dve.wait_ge(fold_mm, 2 * i + 1)
                nc.vector.tensor_copy(ksum_row[:, :], ps[0:1, 0, 0:CH])
                nc.vector.tensor_copy(kxt_sb[:, :, :].rearrange("p h m -> p (h m)"), ps[:, 1, :]).then_inc(fold_in, 1)
                dve.wait_ge(fold_mm, 2 * i + 2)
                for h in range(HALVES):
                    ins = nc.vector.tensor_tensor(kv_w[:, h, :], ps[:, 2, h * P:(h + 1) * P], headmask[:, :], ALU.mult)
                ins.then_inc(fold_in, 1)

                def q_sum(t, par):
                    for h in range(HALVES):
                        dve.wait_ge(ql_ready, 2 * (NB * i + t) + h + 1)
                        nc.vector.scalar_tensor_tensor(q_sb[:, par, h, :], ps[:, QZ_BANK + 2 * par + h, :], 0.0,
                                                       q_act[:, par, h, :], ALU.max, ALU.add).then_inc(q_ready, 1)

                def reciprocals(t):
                    dve.wait_ge(den_mm, NB * i + t + 1)
                    nc.vector.reciprocal(rden[:, :], ps[:, DEN_BANK, 0:P]).then_inc(rden_ready, 1)

                def output(t):
                    dve.wait_ge(num_mm, NB * i + t + 1)
                    dve.wait_ge(wide_evac, 2 * (NB * i + t + 1))
                    nc.vector.tensor_tensor(ratio[:, :, :], ps[:, NUM_BANK:NUM_BANK + 2, :], rden_wide[:, :, :],
                                            ALU.mult).then_inc(num_read, 1)
                    dve.drain()
                    xa = X[:, :, bass.ds(t * BP, BP)]
                    nc.vector.tensor_tensor(xa, ratio[:, :, :], xa, ALU.add).then_inc(out_ready, 1)

                LAG = 4
                q_sum(0, 0)
                reciprocals(0)
                q_sum(1, 1)
                for t in range(1, LAG):
                    output(t - 1)
                    reciprocals(t)
                    q_sum(t + 1, (t + 1) % 2)
                with dve.Fori(LAG // 2, NB // 2 - 1) as j:
                    for t, par in ((2 * j, 0), (2 * j + 1, 1)):
                        output(t - 1)
                        reciprocals(t)
                        q_sum(t + 1, 1 - par)
                        if not last:
                            stat_loaded(i + 1, t - LAG, j - LAG // 2, par)
                for t in (NB - 2, NB - 1):
                    output(t - 1)
                    reciprocals(t)
                    if t == NB - 2:
                        q_sum(NB - 1, 1)
                output(NB - 1)
                if not last:
                    for t in range(NB - 2 - LAG, NB):
                        stat_loaded(i + 1, t, t // 2, t % 2)
                    groupnorm(2 * i + 2)

            images(dve, image)

        @block.tensor
        def _(pe):
            mm = nc.tensor.matmul

            def groupnorm(n):
                pe.wait_ge(gn_in, 3 * n + 1)
                mm(ps[:, GN_BANK, 0:4], gmean[:, :], mean_var[:, :, :].rearrange("p h s -> p (h s)"),
                   start=True, stop=True).then_inc(gn_mm, 1)
                pe.wait_ge(gn_in, 3 * n + 2)
                mm(ps[:, GN_BANK, 4:6], gmean[:, :], gn_dev[:, :], start=True, stop=True).then_inc(gn_mm, 1)

            pe.wait_ge(init_done, 1)
            groupnorm(0)

            def image(i, last):
                def y_of(b, par):
                    pe.wait_ge(xn_ready, NB * i + b + 1)
                    if not first(b, 1):
                        pe.wait_ge(y_evac, NB * i + b)
                    for h in range(HALVES):
                        ins = mm(ps[:, Y_BANK, :].rearrange("p (r c) -> p r c", r=BR), w1_s[:, h, :],
                                 xn[:, par, h, :, 1:1 + COLS], start=(h == 0), stop=(h == HALVES - 1))
                    ins.then_inc(y_mm, 1)

                def fill(b, par, f):
                    if not (first(b, 1) and f < 2):
                        pe.wait_ge(xt_evac, FILLS * (NB * i + b) + f - 1)
                    for c in range(4):
                        n = 4 * f + c
                        r, kw, h = n // 6, n // 2 % 3, n % 2
                        ins = mm(ps[:, XT_BANK + f % 2, c * P:(c + 1) * P], xn[:, par, h, r, kw:kw + COLS], ident[:, :],
                                 start=True, stop=True, is_transpose=True)
                    ins.then_inc(xt_mm, 1)

                def depthwise(b, par):
                    pe.wait_ge(y_halo, NB * i + b + 1)
                    if not first(b, 1):
                        pe.wait_ge(y2_evac, NB * i + b)
                    for k in range(TAPS):
                        kh, kw = divmod(k, KW)
                        ins = mm(ps[:, Y2_BANK, 0:2 * COLS].rearrange("p (r c) -> p r c", r=2), wdiag[:, k, :],
                                 y[:, par, kh:kh + 2, kw:kw + COLS], start=(k == 0), stop=(k == TAPS - 1))
                    ins.then_inc(y2_mm, 1)

                def weights(s, par, r):
                    row = BR * s + r
                    if r == 0:
                        pe.wait_ge(y2_evac, NB * i + s + 1)
                    if not (first(s, 1) and r < 2):
                        pe.wait_ge(mult_done, ROWS * i + row - 1)
                    lo = CR * (r // 2)
                    mm(ps[:, W_BANK + r % 2, 0:NW], ones_bf[:, 0:P], b2_parts[:, :], start=True, stop=False)
                    mm(ps[:, W_BANK + r % 2, 0:NW], y2[lo:lo + CR, par, r % 2, :], w2_s[lo:lo + CR, :],
                       start=False, stop=True).then_inc(w_ready, 1)

                def gather(s, par, r):
                    row = BR * s + r
                    pe.wait_ge(sum_done, ROWS * i + row + 1)
                    if not first(s, 1) and r % 2 == 0:
                        pe.wait_ge(x1_done, PAIRS * i + 2 * s + r // 2 - 1)
                    for h in range(HALVES):
                        o = h * 256 + (r % 2) * P
                        for k in range(KW):
                            ins = mm(ps[:, INV_BANK + r // 2, o:o + P], sums[:, r % 2, k, h * P:(h + 1) * P], ident[:, :],
                                     start=(k == 0), stop=(k == KW - 1), is_transpose=True)
                    ins.then_inc(inv_ready, 1)

                def step(s, par):
                    now, before, nxt, nxt2 = ahead(s, 0), ahead(s, -1), ahead(s, 1), ahead(s, 2)
                    if now:
                        weights(s, par, 0)
                        if before:
                            gather(s - 1, 1 - par, 2)
                    if nxt2:
                        y_of(s + 2, par)
                    if now:
                        weights(s, par, 1)
                    if nxt:
                        fill(s + 1, 1 - par, 0)
                        fill(s + 1, 1 - par, 1)
                    if now:
                        if before:
                            gather(s - 1, 1 - par, 3)
                        weights(s, par, 2)
                    if nxt:
                        fill(s + 1, 1 - par, 2)
                        fill(s + 1, 1 - par, 3)
                    if now:
                        gather(s, par, 0)
                        weights(s, par, 3)
                    if nxt:
                        fill(s + 1, 1 - par, 4)
                        fill(s + 1, 1 - par, 5)
                        depthwise(s + 1, 1 - par)
                    if now:
                        gather(s, par, 1)

                block_steps(pe, step)
                gather(NB - 1, 1, 2)
                gather(NB - 1, 1, 3)
                groupnorm(2 * i + 1)

                pe.wait_ge(w_scaled, i + 1)
                for lo, n, bank in ((0, 512, ROW_BANK), (512, 256, ROW_BANK + 1)):
                    for h in range(HALVES):
                        ins = mm(ps[0:1, bank, 0:n], gn_neg[:, h:h + 1], w_gn[:, h, lo:lo + n],
                                 start=(h == 0), stop=(h == HALVES - 1))
                ins.then_inc(row_mm, 1)

                pe.wait_ge(bias_ready, i + 1)

                def k_of(u, par):
                    pe.wait_ge(xs_ready, PAIRS * i + u + 1)
                    if not first(u, 2):
                        pe.wait_ge(k_ready, PAIRS * i + u - 1)
                    for t in range(2):
                        z = ps[:, KZ_BANK + par, t * CH:(t + 1) * CH]
                        mm(z, ones_bf[:, 0:P], qk_parts[:, CH:2 * CH], start=True, stop=False)
                        for h in range(HALVES):
                            ins = mm(z, xs[:, par, h, t * P:(t + 1) * P], w_gn[:, h, CH:2 * CH], start=False, stop=(h == 1))
                    ins.then_inc(kz_mm, 1)
                    if not first(u, 2):
                        pe.wait_ge(kt_evac, PAIRS * i + u - 1)
                    for t in range(2):
                        for h in range(HALVES):
                            o = t * CH + h * P
                            ins = mm(ps[:, KT_BANK + par, o:o + P], xs[:, par, h, t * P:(t + 1) * P], ident[:, :],
                                     start=True, stop=True, is_transpose=True)
                    ins.then_inc(kt_mm, 1)

                def kx_add(u, par):
                    pe.wait_ge(k_ready, PAIRS * i + u + 1)
                    pe.wait_ge(kt_evac, PAIRS * i + u + 1)
                    for t in range(2):
                        for h in range(HALVES):
                            ins = mm(ps[:, KX_BANK + h, 0:XO], k_sb[:, par, t, h * P:(h + 1) * P], xt_sb[:, par, t, :],
                                     start=(first(u, 1) and t == 0), stop=(isinstance(u, int) and u == PAIRS - 1 and t == 1))
                    ins.then_inc(kx_done, 1)

                k_of(0, 0)
                k_of(1, 1)
                kx_add(0, 0)
                with pe.Fori(1, PAIRS // 2) as j:
                    k_of(2 * j, 0)
                    kx_add(2 * j - 1, 1)
                    k_of(2 * j + 1, 1)
                    kx_add(2 * j, 0)
                kx_add(PAIRS - 1, 1)

                pe.wait_ge(fold_in, 3 * i + 1)
                for h in range(HALVES):
                    mm(ps[0:1, 0, h * P:(h + 1) * P], kx_sb[:, h, CH:XO], ident[:, :], start=True, stop=True)
                for ih in range(HALVES):
                    for h in range(HALVES):
                        o = ih * CH + h * P
                        ins = mm(ps[:, 1, o:o + P], kx_sb[:, h, ih * P:(ih + 1) * P], ident[:, :],
                                 start=True, stop=True, is_transpose=True)
                ins.then_inc(fold_mm, 1)
                pe.wait_ge(fold_in, 3 * i + 2)
                for h in range(HALVES):
                    kv = ps[:, 2, h * P:(h + 1) * P]
                    for ih in range(HALVES):
                        mm(kv, kxt_sb[:, ih, h * P:(h + 1) * P], w_gn[:, ih, 2 * CH + h * P:2 * CH + (h + 1) * P],
                           start=(ih == 0), stop=False)
                    ins = mm(kv, ksum_row[:, h * P:(h + 1) * P], bias_row[:, 2 * CH + h * P:2 * CH + (h + 1) * P],
                             start=False, stop=True)
                ins.then_inc(fold_mm, 1)

                pe.wait_ge(fold_in, 3 * i + 3)

                def q_of(t, par, h):
                    if not first(t, 2):
                        pe.wait_ge(q_ready, 2 * (NB * i + t) + h - 3)
                    z = ps[:, QZ_BANK + 2 * par + h, :]
                    mm(z, qk_parts[:, h * P:(h + 1) * P], ones_bf[:, :], start=True, stop=False)
                    for ih in range(HALVES):
                        ins = mm(z, w_gn[:, ih, h * P:(h + 1) * P], X[:, ih, bass.ds(t * BP, BP)], start=False, stop=(ih == 1))
                    ins.then_inc(qz_mm, 1)

                def denominators(t, par):
                    pe.wait_ge(q_ready, 2 * (NB * i + t) + 2)
                    if not first(t, 1):
                        pe.wait_ge(wide_evac, 2 * (NB * i + t))
                    for h in range(HALVES):
                        for c in range(BR):
                            ins = mm(ps[32 * c:32 * c + DEN_COLS, DEN_BANK, 0:P], den_w[:, h, :],
                                     q_sb[:, par, h, c * P:(c + 1) * P], start=(h == 0), stop=(h == 1),
                                     tile_position=(0, 32 * c))
                    ins.then_inc(den_mm, 1)

                def numerators(t, par):
                    if not first(t, 1):
                        pe.wait_ge(num_read, NB * i + t)
                    for h in range(HALVES):
                        ins = mm(ps[:, NUM_BANK + h, :], kv_w[:, h, :], q_sb[:, par, h, :], start=True, stop=True)
                    ins.then_inc(num_mm, 1)

                def widen(t):
                    pe.wait_ge(rden_ready, NB * i + t + 1)
                    for h in range(HALVES):
                        for c in range(BR):
                            ins = mm(ps[:, WIDE_BANK[h], c * P:(c + 1) * P], headsel[:, c, h, :], rden[:, :],
                                     start=True, stop=True)
                        ins.then_inc(wide_mm, 1)

                def c_step(t, par, more):
                    if more:
                        q_of(t + 1, 1 - par, 0)
                    denominators(t, par)
                    if more:
                        q_of(t + 1, 1 - par, 1)
                    numerators(t, par)
                    widen(t)

                pe.wait_ge(sel_loaded, 16 * (i + 1))
                q_of(0, 0, 0)
                q_of(0, 0, 1)
                c_step(0, 0, True)
                c_step(1, 1, True)
                with pe.Fori(1, NB // 2 - 1) as j:
                    c_step(2 * j, 0, True)
                    c_step(2 * j + 1, 1, True)
                c_step(NB - 2, 0, True)
                c_step(NB - 1, 1, False)
                if not last:
                    groupnorm(2 * i + 2)

            images(pe, image)


_OUT = "out_dram"


def kernel(**inputs):
    import numpy as np
    import concourse.bacc as bacc
    from concourse.bass_utils import run_bass_kernel_spmd

    a = {k: np.asarray(v) for k, v in inputs.items()}
    w1t = a["L0_conv_w1"].T
    w2t = a["L0_conv_w2"].reshape(GROUPS, TAPS, CR).transpose(2, 1, 0).reshape(CR, NW)
    arrays = {
        "x": a["x"],
        "w1t": np.concatenate([w1t, w1t], axis=1),
        "b1": np.concatenate([a["L0_conv_b1"]] * 2).reshape(P, 1),
        "wd": np.concatenate([a["L0_conv_wd"].reshape(CR, TAPS)] * 2),
        "bd": np.concatenate([a["L0_conv_bd"]] * 2).reshape(P, 1),
        "w2t": np.concatenate([w2t, w2t]),
        "b2": a["L0_conv_b2"].reshape(GROUPS, TAPS).T.reshape(1, NW),
        "wqkv": np.concatenate([a["L1_conv_Wq"].T, a["L1_conv_Wk"].T, a["L1_conv_Wv"].T], axis=1),
        "bqkv": np.concatenate([a["L1_conv_bq"], a["L1_conv_bk"], a["L1_conv_bv"]]).reshape(1, 3 * CH),
    }
    c = np.arange(P)
    head = c[:, None] // 32 + 4 * np.arange(HALVES)[None, :]
    sel = (head[:, :, None] == (np.arange(DEN_COLS) % HEADS)[None, None, :]).astype(np.float32)
    once = (sel * (np.arange(DEN_COLS) < HEADS)).transpose(2, 1, 0)[:, None]
    arrays.update({
        "ident": np.eye(P, dtype=np.float32),
        "gmean": ((c[:, None] // 8 == c[None, :] // 8) / 8.0).astype(np.float32),
        "headmask": (c[:, None] // 32 == c[None, :] // 32).astype(np.float32),
        "densel": sel,
        "headsel": np.concatenate([once * (np.arange(BR) == q)[None, :, None, None] for q in range(BR)]).astype(np.float32),
    })
    arrays = {f"{k}_in": np.ascontiguousarray(v) for k, v in arrays.items()}
    nc = bacc.Bacc("TRN2", target_bir_lowering=False, num_devices=1)
    args = [nc.dram_tensor(k, v.shape, mybir.dt.from_np(v.dtype), kind="ExternalInput").ap() for k, v in arrays.items()]
    args.append(nc.dram_tensor(_OUT, (IMAGES, CH, ROWS, COLS), F32, kind="ExternalOutput").ap())
    two_block_kernel(nc, *args)
    r = run_bass_kernel_spmd(nc, [arrays], core_ids=[0])
    return r.results[0][_OUT]
```

```python
from contextlib import ExitStack

import concourse.bass as bass
from concourse import mybir

F32 = mybir.dt.float32
BF16 = mybir.dt.bfloat16
FP16 = mybir.dt.float16
I32 = mybir.dt.int32
ALU = mybir.AluOpType
ACT = mybir.ActivationFunctionType

P = 128
IMAGES, CH, ROWS, COLS = 8, 256, 128, 128
HALVES = CH // P
PIX = ROWS * COLS
TAPS = 9
KW = 3
GROUPS = 16
GC = CH // GROUPS
CR = 64
NW = TAPS * GROUPS
BR = 4
NB = ROWS // BR
BP = BR * COLS
PADW = COLS + 2
RING = 8
ROWT = KW * CH
FILLS = BR * KW * HALVES // 4
PAIRS = ROWS // 2
HEADS = 8
GN_EPS = 1e-5
KSUM_EPS = 1e-6
EXPONENT = 0x7F800000
TINY = 1e-30
W_RANGE = 512.0
BIAS_ROWS = 96
PARTS = 3
DEN_COLS = 32


def two_block_kernel(nc, x, w1t, b1, wd, bd, w2t, b2, wk, bk, wqv_in, bqv, ident_in, gmean_in, headmask_in, densel_in, partsel_in, headsel_in, out):
    x_v = x.rearrange("b (h p) r c -> b p h (r c)", p=P)
    out_v = out.rearrange("b (h p) r c -> b p h (r c)", p=P)

    with ExitStack() as ctx:
        def sb(name, shape, dt=F32):
            return ctx.enter_context(nc.sbuf_tensor(name, shape, dt))

        def sem(name):
            return ctx.enter_context(nc.semaphore(name))

        X = sb("X", [P, HALVES, PIX])
        w1_s = sb("w1_s", [P, HALVES, P])
        b1_s = sb("b1_s", [P, 1])
        wd_s = sb("wd_s", [P, TAPS])
        wdiag = sb("wdiag", [P, TAPS, P])
        zero_row = sb("zero_row", [P, PADW])
        bd_s = sb("bd_s", [P, 1])
        w2_s = sb("w2_s", [P, NW])
        wk_parts = sb("wk_parts", [P, 2, HALVES, CH], FP16)
        k_unscale = sb("k_unscale", [P, 2])
        bqv_row = sb("bqv_row", [1, 2 * CH])
        ident = sb("ident", [P, P])
        gmean = sb("gmean", [P, P])
        headmask = sb("headmask", [P, P])
        densel = sb("densel", [P, HALVES, DEN_COLS])
        partsel = sb("partsel", [P, 2])
        ones_bf = sb("ones_bf", [BIAS_ROWS, BP], BF16)
        b2_parts = sb("b2_parts", [BIAS_ROWS, NW], BF16)
        k_parts = sb("k_parts", [BIAS_ROWS, CH], BF16)
        q_parts = sb("q_parts", [BIAS_ROWS, CH], BF16)

        stats = sb("stats", [P, HALVES, NB, 6])
        mean_var = sb("mean_var", [P, HALVES, 2])
        gn_mean = sb("gn_mean", [P, 2])
        gn_avg = sb("gn_avg", [P, 2])
        gn_dev = sb("gn_dev", [P, 2])
        gn_var = sb("gn_var", [P, 2])
        gn_ln = sb("gn_ln", [P, 2])
        gn_r0 = sb("gn_r0", [P, 2])
        gn_t = sb("gn_t", [P, 2])
        gn_rstd = sb("gn_rstd", [P, 2])
        gn_shift = sb("gn_shift", [P, 2])
        gn_neg = sb("gn_neg", [P, 2])

        xn = sb("xn", [P, 2, HALVES, BR, PADW])
        y = sb("y", [P, 2, BR, PADW])
        y_last = sb("y_last", [CR, COLS])
        y2 = sb("y2", [P, 2, 2, COLS])
        place = sb("place", [P, 2 * KW * CH])
        sums = place[:, :].rearrange("p (s k c) -> p s k c", s=2, k=KW)
        wqv = place[:, 0:HALVES * 2 * CH].rearrange("p (h m) -> p h m", h=HALVES)
        arena = sb("arena", [P, RING * ROWT + 2 * TAPS * CH])
        xt = arena[:, 0:RING * ROWT]
        prod = arena[:, RING * ROWT:].rearrange("p (s k c) -> p s k c", s=2, k=TAPS)

        at = [0]

        def piece(n):
            at[0] += n
            return arena[:, at[0] - n:at[0]]

        xs = piece(2 * HALVES * 2 * P).rearrange("p (s h n) -> p s h n", s=2, h=HALVES)
        k_act = piece(2 * 2 * CH).rearrange("p (s n) -> p s n", s=2)
        k_sb = piece(2 * 2 * CH).rearrange("p (s t m) -> p s t m", s=2, t=2)
        XO = CH + 1
        xt_sb = piece(2 * 2 * XO).rearrange("p (s t m) -> p s t m", s=2, t=2)
        kx_sb = piece(HALVES * XO).rearrange("p (h m) -> p h m", h=HALVES)
        kxt_sb = piece(HALVES * CH).rearrange("p (h m) -> p h m", h=HALVES)
        x_parts = piece(2 * 2 * HALVES * 2 * P // 2).bitcast(FP16).rearrange("p (s n h m) -> p s n h m", s=2, n=2, h=HALVES)
        wk_raw = piece(HALVES * CH).rearrange("p (h m) -> p h m", h=HALVES)
        one_row = piece(P)[0:1, :]
        bk_row = piece(CH)[0:1, :]
        bias_row = piece(CH)[0:1, :]
        ksum_row = piece(CH)[0:1, :]
        b2_row = piece(NW)[0:1, :]
        part_rest = piece(CH)[0:1, :]
        part_mid = piece(CH)[0:1, :].bitcast(BF16)[:, 0:CH]
        kv_w = piece(HALVES * P).rearrange("p (h n) -> p h n", h=HALVES)
        den_w = piece(HALVES * DEN_COLS).rearrange("p (h n) -> p h n", h=HALVES)
        fold_start = at[0] - HALVES * (P + DEN_COLS)
        headsel = piece(BR * HALVES * P // 2).bitcast(BF16).rearrange("p (c h n) -> p c h n", c=BR, h=HALVES)
        assert at[0] <= RING * ROWT + 2 * TAPS * CH
        at[0] = 0
        q_act = piece(2 * HALVES * BP).rearrange("p (s h n) -> p s h n", s=2, h=HALVES)
        q_sb = piece(2 * HALVES * BP).rearrange("p (s h n) -> p s h n", s=2, h=HALVES)
        rden_wide = piece(HALVES * BP).rearrange("p (h n) -> p h n", h=HALVES)
        ratio = piece(HALVES * BP).rearrange("p (h n) -> p h n", h=HALVES)
        rden = piece(P)
        rden_rest = piece(P)
        rden_high = piece(P // 2).bitcast(BF16)
        rden_parts = piece(P // 2).bitcast(BF16)
        assert at[0] <= fold_start

        ksum_eps = sb("ksum_eps", [P, HALVES])
        w_max = sb("w_max", [P, 1])
        w_pow = sb("w_pow", [1, 2])

        ps = ctx.enter_context(nc.psum_tensor("ps", [P, 8, 512], F32))
        XT_BANK, W_BANK, INV_BANK = 0, 4, 6
        Y_BANK, Y2_BANK = 2, 3
        KZ_BANK, KT_BANK, KX_BANK = 0, 2, 4
        QZ_BANK, NUM_BANK, DEN_BANK, WIDE_BANK = 0, 4, 6, (7, 6)
        GN_BANK, ROW_BANK = 2, 6

        const_loaded = sem("const_loaded")
        sel_loaded = sem("sel_loaded")
        w_loaded = sem("w_loaded")
        x_loaded = [sem("x_loaded0"), sem("x_loaded1")]
        out_stored = [sem("out_stored0"), sem("out_stored1")]
        init_done = sem("init_done")
        gn_in = sem("gn_in")
        gn_mm = sem("gn_mm")
        gn_root = sem("gn_root")
        gn_ready = sem("gn_ready")
        xn_ready = sem("xn_ready")
        y_mm = sem("y_mm")
        y_halo = sem("y_halo")
        y_evac = sem("y_evac")
        y2_mm = sem("y2_mm")
        y2_evac = sem("y2_evac")
        xt_mm = sem("xt_mm")
        xt_evac = sem("xt_evac")
        w_ready = sem("w_ready")
        mult_two = sem("mult_two")
        mult_done = sem("mult_done")
        sum_two = sem("sum_two")
        sum_done = sem("sum_done")
        last_used = sem("last_used")
        inv_ready = sem("inv_ready")
        x1_done = sem("x1_done")
        w_max_in = sem("w_max_in")
        w_max_mm = sem("w_max_mm")
        w_scaled = sem("w_scaled")
        row_mm = sem("row_mm")
        bias_ready = sem("bias_ready")
        xs_ready = sem("xs_ready")
        kz_mm = sem("kz_mm")
        kt_mm = sem("kt_mm")
        kl_ready = sem("kl_ready")
        kt_evac = sem("kt_evac")
        k_ready = sem("k_ready")
        kx_done = sem("kx_done")
        fold_in = sem("fold_in")
        fold_mm = sem("fold_mm")
        qz_mm = sem("qz_mm")
        ql_ready = sem("ql_ready")
        q_ready = sem("q_ready")
        den_mm = sem("den_mm")
        rden_ready = sem("rden_ready")
        num_mm = sem("num_mm")
        wide_mm = sem("wide_mm")
        wide_evac = sem("wide_evac")
        num_read = sem("num_read")
        out_ready = sem("out_ready")

        N_CONST = 14
        block = ctx.enter_context(nc.Block())

        def images(eng, image):
            with eng.Fori(0, IMAGES - 1) as i:
                image(i, False)
            image(IMAGES - 1, True)

        def block_steps(eng, step):
            for s in range(-2, 2):
                step(s, s % 2)
            with eng.Fori(1, NB // 2 - 2) as j:
                step(2 * j, 0)
                step(2 * j + 1, 1)
            for s in range(NB - 4, NB):
                step(s, s % 2)

        def ahead(s, n):
            return not isinstance(s, int) or 0 <= s + n < NB

        def first(s, n):
            return isinstance(s, int) and s < n

        @block.sync
        def _(sp):
            for dst, src in ((w1_s[:, :, :], w1t.rearrange("(h p) n -> p h n", p=P)), (b1_s[:, :], b1), (wd_s[:, :], wd),
                             (bd_s[:, :], bd), (w2_s[:, :], w2t), (b2_row[:, :], b2),
                             (bqv_row[:, :], bqv), (wk_raw, wk.rearrange("(h p) n -> p h n", p=P)), (bk_row, bk),
                             (ident[:, :], ident_in), (gmean[:, :], gmean_in), (headmask[:, :], headmask_in),
                             (densel[:, :, :], densel_in), (partsel[:, :], partsel_in)):
                sp.dma_start(dst, src).then_inc(const_loaded, 16)

            def load(i, t, par):
                sp.dma_start(X[:, :, bass.ds(t * BP, BP)], x_v[i, :, :, bass.ds(t * BP, BP)]).then_inc(x_loaded[par], 16)

            load(0, 0, 0)
            load(0, 1, 1)
            with sp.Fori(1, NB // 2) as j:
                sp.wait_ge(x_loaded[0], 16 * j)
                load(0, 2 * j, 0)
                sp.wait_ge(x_loaded[1], 16 * j)
                load(0, 2 * j + 1, 1)

            def image(i, last):
                def store(t, par):
                    sp.wait_ge(out_ready, NB * i + t + 1)
                    sp.dma_start(out_v[i, :, :, bass.ds(t * BP, BP)], X[:, :, bass.ds(t * BP, BP)]).then_inc(out_stored[par], 16)

                def next_load(t_half, par):
                    if not last:
                        sp.wait_ge(out_stored[par], 16 * (NB // 2 * i + t_half + 1))
                        sp.wait_ge(x_loaded[par], 16 * (NB // 2 * (i + 1) + t_half))
                        load(i + 1, 2 * t_half + par, par)

                sp.wait_ge(x1_done, PAIRS * (i + 1))
                sp.dma_start(wqv, wqv_in.rearrange("(h p) n -> p h n", p=P)).then_inc(w_loaded, 16)
                sp.wait_ge(gn_ready, 2 * i + 2)
                sp.dma_start(headsel, headsel_in).then_inc(sel_loaded, 16)
                store(0, 0)
                store(1, 1)
                next_load(0, 0)
                with sp.Fori(1, NB // 2) as j:
                    store(2 * j, 0)
                    next_load(j - 1, 1)
                    store(2 * j + 1, 1)
                    next_load(j, 0)
                next_load(NB // 2 - 1, 1)

            images(sp, image)
            for par in range(2):
                sp.wait_ge(out_stored[par], 16 * (NB // 2) * IMAGES)

        @block.gpsimd
        def _(pool):
            def image(i, last):
                def add_products(s, r):
                    row = BR * s + r
                    pool.wait_ge(mult_two, ROWS * i + row + 1)
                    if not (first(s, 1) and r < 2):
                        pool.wait_ge(inv_ready, ROWS * i + row - 1)
                    nc.gpsimd.tensor_tensor(sums[:, r % 2, :, :], prod[:, r % 2, 0:KW, :], prod[:, r % 2, KW:2 * KW, :],
                                            ALU.add).then_inc(sum_two, 1)
                    pool.wait_ge(mult_done, ROWS * i + row + 1)
                    pool.wait_ge(sum_two, ROWS * i + row + 1)
                    nc.gpsimd.tensor_tensor(sums[:, r % 2, 0:KW - 1, :], sums[:, r % 2, 0:KW - 1, :],
                                            prod[:, r % 2, 2 * KW:TAPS - 1, :], ALU.add).then_inc(sum_done, 1)

                for r in range(BR):
                    add_products(0, r)
                with pool.Fori(1, NB) as s:
                    for r in range(BR):
                        add_products(s, r)

                def add_output(t):
                    xa = X[:, :, bass.ds(t * BP, BP)]
                    pool.wait_ge(num_read, NB * i + t + 1)
                    nc.gpsimd.tensor_tensor(xa, ratio[:, :, :], xa, ALU.add).then_inc(out_ready, 1)

                with pool.Fori(0, NB) as t:
                    add_output(t)

            images(pool, image)

        @block.scalar
        def _(act):
            def gn_guess(n):
                act.wait_ge(gn_in, 3 * n + 3)
                nc.scalar.activation(gn_ln[:, :], gn_var[:, :], ACT.Ln)
                act.drain()
                nc.scalar.activation(gn_r0[:, :], gn_ln[:, :], ACT.Exp, scale=-0.5).then_inc(gn_root, 1)

            def normalise(i, b, par):
                if not first(b, 2):
                    act.wait_ge(xt_mm, FILLS * (NB * i + b - 1))
                for h in range(HALVES):
                    ins = nc.scalar.activation(
                        xn[:, par, h, :, 1:1 + COLS], X[:, h, bass.ds(b * BP, BP)].rearrange("p (r c) -> p r c", r=BR),
                        ACT.Identity, bias=gn_shift[:, h:h + 1], scale=gn_rstd[:, h:h + 1])
                ins.then_inc(xn_ready, 1)

            def y_out(i, b, par):
                act.wait_ge(y_mm, NB * i + b + 1)
                yp = ps[:, Y_BANK, :].rearrange("p (r c) -> p r c", r=BR)

                def put(lo, dst, src):
                    return nc.scalar.activation(dst, src, ACT.Identity, bias=b1_s[lo:lo + CR, :])

                if first(b, 1):
                    nc.scalar.copy(y[0:CR, par, 0, :], zero_row[0:CR, :])
                else:
                    put(CR, y[CR:P, 1 - par, BR - 1:BR, 1:1 + COLS], yp[CR:P, 0:1, :]).then_inc(y_halo, 1)
                    nc.scalar.copy(y[0:CR, par, 0, 1:1 + COLS], y_last[:, :])
                put(0, y[0:CR, par, 1:BR, 1:1 + COLS], yp[0:CR, 0:BR - 1, :])
                put(CR, y[CR:P, par, 0:BR - 1, 1:1 + COLS], yp[CR:P, 1:BR, :])
                if not (isinstance(b, int) and b == 0):
                    act.drain()
                put(0, y_last[:, :], yp[0:CR, BR - 1, :]).then_inc(y_evac, 1)
                if isinstance(b, int) and b == NB - 1:
                    nc.scalar.copy(y[CR:P, par, BR - 1, :], zero_row[CR:P, :]).then_inc(y_halo, 1)

            def y2_out(i, b, par):
                act.wait_ge(y2_mm, NB * i + b + 1)
                nc.scalar.activation(y2[:, par, :, :], ps[:, Y2_BANK, 0:2 * COLS].rearrange("p (r c) -> p r c", r=2),
                                     ACT.Identity, bias=bd_s[:, :]).then_inc(y2_evac, 1)

            def xt_out(i, b, par):
                if not first(b, 1):
                    act.wait_ge(mult_done, ROWS * i + BR * b - 3)
                for f in range(FILLS):
                    act.wait_ge(xt_mm, FILLS * (NB * i + b) + f + 1)
                    o = par * BR * ROWT + f * 512
                    nc.scalar.copy(xt[:, o:o + 512], ps[:, XT_BANK + f % 2, :]).then_inc(xt_evac, 1)

            def softplus_log(dst, z, scale=1.0):
                nc.scalar.activation(dst, z, ACT.Abs, scale=scale)
                act.drain()
                nc.scalar.activation(dst, dst, ACT.Exp, scale=-1.0)
                act.drain()
                return nc.scalar.activation(dst, dst, ACT.Ln, bias=1.0)

            nc.scalar.preload_act_table_set("natural_log_exp_and_others")
            act.wait_ge(init_done, 1)
            gn_guess(0)

            def image(i, last):
                act.wait_ge(gn_ready, 2 * i + 1)
                normalise(i, 0, 0)

                def step(s, par):
                    if ahead(s, 2):
                        y_out(i, s + 2, par)
                    if ahead(s, 1):
                        xt_out(i, s + 1, 1 - par)
                        y2_out(i, s + 1, 1 - par)
                    if ahead(s, 3):
                        normalise(i, s + 3, 1 - par)

                block_steps(act, step)
                gn_guess(2 * i + 1)

                def k_pair(u, par):
                    act.wait_ge(kz_mm, PAIRS * i + u + 1)
                    if not first(u, 2):
                        act.wait_ge(k_ready, PAIRS * i + u - 1)
                    softplus_log(k_act[:, par, :], ps[:, KZ_BANK + par, :], k_unscale[:, 1:2]).then_inc(kl_ready, 1)
                    act.wait_ge(kt_mm, PAIRS * i + u + 1)
                    if not first(u, 2):
                        act.wait_ge(kx_done, PAIRS * i + u - 1)
                    nc.scalar.copy(xt_sb[:, par, :, 0:CH], ps[:, KT_BANK + par, :].rearrange("p (t m) -> p t m", t=2)
                                   ).then_inc(kt_evac, 1)

                k_pair(0, 0)
                k_pair(1, 1)
                with act.Fori(1, PAIRS // 2) as j:
                    k_pair(2 * j, 0)
                    k_pair(2 * j + 1, 1)

                def q_log(t, par):
                    for h in range(HALVES):
                        act.wait_ge(qz_mm, 2 * (NB * i + t) + h + 1)
                        softplus_log(q_act[:, par, h, :], ps[:, QZ_BANK + 2 * par + h, :]).then_inc(ql_ready, 1)

                def wide_out(t):
                    for h in range(HALVES):
                        act.wait_ge(wide_mm, 2 * (NB * i + t) + h + 1)
                        if h == 0 and not first(t, 1):
                            act.wait_ge(num_read, NB * i + t)
                        nc.scalar.copy(rden_wide[:, h, :], ps[:, WIDE_BANK[h], :]).then_inc(wide_evac, 1)

                q_log(0, 0)
                q_log(1, 1)
                wide_out(0)
                with act.Fori(1, NB // 2) as j:
                    q_log(2 * j, 0)
                    wide_out(2 * j - 1)
                    q_log(2 * j + 1, 1)
                    wide_out(2 * j)
                wide_out(NB - 1)
                if not last:
                    gn_guess(2 * i + 2)

            images(act, image)

        @block.vector
        def _(dve):
            def stat(t):
                for h in range(HALVES):
                    nc.vector.bn_stats(stats[:, h, bass.ds(t, 1), :], X[:, h, bass.ds(t * BP, BP)])

            def stat_loaded(n, t, t_half, par):
                dve.wait_ge(x_loaded[par], 16 * (NB // 2 * n + t_half + 1))
                stat(t)

            def groupnorm(n):
                dve.drain()
                for h in range(HALVES):
                    ins = nc.vector.bn_aggr(mean_var[:, h, :], stats[:, h, :, :].rearrange("p t s -> p (t s)"))
                ins.then_inc(gn_in, 1)
                dve.wait_ge(gn_mm, 2 * n + 1)
                means = ps[:, GN_BANK, 0:4].rearrange("p (h s) -> p h s", h=2)
                nc.vector.tensor_copy(gn_mean[:, :], means[:, :, 0])
                nc.vector.tensor_copy(gn_avg[:, :], means[:, :, 1])
                dve.drain()
                nc.vector.tensor_tensor(gn_dev[:, :], mean_var[:, :, 0], gn_mean[:, :], ALU.subtract)
                dve.drain()
                nc.vector.tensor_tensor(gn_dev[:, :], gn_dev[:, :], gn_dev[:, :], ALU.mult).then_inc(gn_in, 1)
                dve.wait_ge(gn_mm, 2 * n + 2)
                nc.vector.scalar_tensor_tensor(gn_var[:, :], ps[:, GN_BANK, 4:6], GN_EPS, gn_avg[:, :],
                                               ALU.add, ALU.add).then_inc(gn_in, 1)
                dve.wait_ge(gn_root, n + 1)
                nc.vector.tensor_tensor(gn_t[:, :], gn_r0[:, :], gn_r0[:, :], ALU.mult)
                dve.drain()
                nc.vector.tensor_tensor(gn_t[:, :], gn_t[:, :], gn_var[:, :], ALU.mult)
                dve.drain()
                nc.vector.tensor_scalar(gn_t[:, :], gn_t[:, :], -0.5, 1.5, ALU.mult, ALU.add)
                dve.drain()
                nc.vector.tensor_tensor(gn_rstd[:, :], gn_r0[:, :], gn_t[:, :], ALU.mult)
                dve.drain()
                nc.vector.tensor_scalar(gn_neg[:, :], gn_mean[:, :], -1.0, None, ALU.mult)
                nc.vector.scalar_tensor_tensor(gn_shift[:, :], gn_mean[:, :], -1.0, gn_rstd[:, :],
                                               ALU.mult, ALU.mult).then_inc(gn_ready, 1)

            def in_parts(parts, row, n):
                dve.drain()
                nc.vector.tensor_copy(parts[0:1, 0:n], row)
                dve.drain()
                nc.vector.tensor_tensor(part_rest[:, 0:n], row, parts[0:1, 0:n], ALU.subtract)
                dve.drain()
                nc.vector.tensor_copy(part_mid[:, 0:n], part_rest[:, 0:n])
                dve.drain()
                nc.vector.tensor_copy(parts[32:33, 0:n], part_mid[:, 0:n])
                nc.vector.tensor_tensor(part_rest[:, 0:n], part_rest[:, 0:n], part_mid[:, 0:n], ALU.subtract)
                dve.drain()
                return nc.vector.tensor_copy(parts[64:65, 0:n], part_rest[:, 0:n])

            nc.vector.memset(xn[:, :, :, :, :], 0.0)
            nc.vector.memset(y[:, :, :, :], 0.0)
            nc.vector.memset(b2_parts[:, :], 0.0)
            nc.vector.memset(k_parts[:, :], 0.0)
            nc.vector.memset(q_parts[:, :], 0.0)
            nc.vector.memset(one_row, 1.0)
            nc.vector.memset(ones_bf[:, :], 1.0)
            nc.vector.memset(zero_row[:, :], 0.0)
            dve.wait_ge(const_loaded, 16 * N_CONST)
            for k in range(TAPS):
                nc.vector.tensor_scalar(wdiag[:, k, :], ident[:, :], wd_s[:, k:k + 1], None, ALU.mult)
            in_parts(b2_parts, b2_row[:, :], NW).then_inc(init_done, 1)

            nc.vector.tensor_reduce(w_max[:, :], wk_raw.rearrange("p h m -> p (h m)"), mybir.AxisListType.X, ALU.max,
                                    apply_absolute_value=True).then_inc(w_max_in, 1)
            dve.wait_ge(w_max_mm, 1)
            nc.vector.tensor_reduce(w_pow[:, 0:1], ps[0:1, GN_BANK, 0:P], mybir.AxisListType.X, ALU.max)
            dve.drain()
            nc.vector.tensor_scalar(w_pow[:, 0:1], w_pow[:, 0:1], TINY, None, ALU.max)
            dve.drain()
            nc.vector.tensor_scalar(w_pow[:, 0:1].bitcast(I32), w_pow[:, 0:1].bitcast(I32), EXPONENT, None, ALU.bitwise_and)
            dve.drain()
            nc.vector.tensor_scalar(w_pow[:, 1:2], w_pow[:, 0:1], 1.0 / W_RANGE, None, ALU.mult)
            dve.drain()
            nc.vector.reciprocal(w_pow[:, 0:1], w_pow[:, 1:2]).then_inc(w_max_in, 1)
            dve.wait_ge(w_max_mm, 2)
            nc.vector.tensor_copy(k_unscale[:, :], ps[:, GN_BANK, 0:2])
            dve.drain()
            nc.vector.tensor_scalar(wk_raw, wk_raw, k_unscale[:, 0:1], None, ALU.mult)
            nc.vector.tensor_scalar(bk_row, bk_row, k_unscale[0:1, 0:1], None, ALU.mult)
            dve.drain()
            nc.vector.tensor_copy(wk_parts[:, 0, :, :], wk_raw)
            dve.drain()
            nc.vector.tensor_tensor(wk_parts[:, 1, :, :], wk_raw, wk_parts[:, 0, :, :], ALU.subtract)
            in_parts(k_parts, bk_row, CH)
            with dve.Fori(0, NB // 2) as j:
                stat_loaded(0, 2 * j, j, 0)
                stat_loaded(0, 2 * j + 1, j, 1)
            groupnorm(0)

            def image(i, last):
                def products(s, par, r):
                    row = BR * s + r
                    dve.wait_ge(w_ready, ROWS * i + row + 1)
                    if not (first(s, 1) and r < 2):
                        dve.wait_ge(sum_done, ROWS * i + row - 1)
                    for kh in range(KW):
                        if kh == 2 and not (isinstance(s, int) and s == NB - 1 and r == BR - 1):
                            fills = (3, 5, 6, FILLS + 2)[r]
                            dve.wait_ge(xt_evac, FILLS * (NB * i + s) + fills)
                        if kh == 2 and not (first(s, 1) and r < 2):
                            dve.wait_ge(last_used, ROWS * i + row - 1)
                        slot = (BR * par + r + kh - 1) % RING
                        ins = nc.vector.tensor_tensor(
                            prod[:, r % 2, KW * kh:KW * kh + KW, :].rearrange("p k (g c) -> p (k g) c", c=GC),
                            ps[:, W_BANK + r % 2, 48 * kh:48 * kh + 48].unsqueeze(2).to_broadcast([P, 48, GC]),
                            xt[:, slot * ROWT:(slot + 1) * ROWT].rearrange("p (a c) -> p a c", c=GC), ALU.mult)
                        if kh == 1:
                            ins.then_inc(mult_two, 1)
                    ins.then_inc(mult_done, 1)

                def add_rows(s, pair):
                    q = 2 * s + pair
                    dve.wait_ge(inv_ready, ROWS * i + 2 * q + 2)
                    xa = X[:, :, bass.ds(q * 2 * COLS, 2 * COLS)]
                    nc.vector.tensor_tensor(xa, ps[:, INV_BANK + pair, :].rearrange("p (h n) -> p h n", h=2), xa,
                                            ALU.add).then_inc(x1_done, 1)

                def step(s, par):
                    if not ahead(s, 0):
                        return
                    products(s, par, 0)
                    products(s, par, 1)
                    if not first(s, 1):
                        add_rows(s - 1, 1)
                    products(s, par, 2)
                    if not first(s, 1):
                        dve.drain()
                        stat(s - 1)
                    if isinstance(s, int) and s == NB - 1:
                        nc.vector.memset(xt[:, 0:ROWT], 0.0)
                        dve.drain()
                    products(s, par, 3)
                    add_rows(s, 0)

                nc.vector.memset(xt[:, (RING - 1) * ROWT:RING * ROWT], 0.0)
                dve.drain()
                block_steps(dve, step)
                add_rows(NB - 1, 1)
                dve.drain()
                stat(NB - 1)
                groupnorm(2 * i + 1)

                nc.vector.memset(xt_sb[:, :, :, CH:XO], 1.0)

                def split_x(u, par):
                    if not first(u, 2):
                        dve.wait_ge(kt_mm, PAIRS * i + u - 1)
                    for h in range(HALVES):
                        nc.vector.tensor_scalar(xs[:, par, h, :], X[:, h, bass.ds(u * 2 * COLS, 2 * COLS)],
                                                gn_rstd[:, h:h + 1], gn_shift[:, h:h + 1], ALU.mult, ALU.add)
                    dve.drain()
                    nc.vector.tensor_copy(x_parts[:, par, 0, :, :], xs[:, par, :, :])
                    dve.drain()
                    nc.vector.tensor_tensor(x_parts[:, par, 1, :, :], xs[:, par, :, :], x_parts[:, par, 0, :, :],
                                            ALU.subtract).then_inc(xs_ready, 1)

                def k_sum(u, par):
                    dve.wait_ge(kl_ready, PAIRS * i + u + 1)
                    if not first(u, 2):
                        dve.wait_ge(kx_done, PAIRS * i + u - 1)
                    k = k_sb[:, par, :, :].rearrange("p t m -> p (t m)")
                    nc.vector.tensor_scalar(k, ps[:, KZ_BANK + par, :], k_unscale[:, 1:2], 0.0, ALU.mult, ALU.max)
                    dve.drain()
                    nc.vector.tensor_tensor(k, k, k_act[:, par, :], ALU.add).then_inc(k_ready, 1)

                dve.drain()
                split_x(0, 0)
                split_x(1, 1)
                dve.wait_ge(w_loaded, 16 * (i + 1))
                for h in range(HALVES):
                    ins = nc.vector.tensor_scalar(wqv[:, h, 0:CH], wqv[:, h, 0:CH], gn_rstd[:, h:h + 1], None, ALU.mult)
                ins.then_inc(w_scaled, 1)
                k_sum(0, 0)
                dve.wait_ge(row_mm, i + 1)
                nc.vector.tensor_tensor(bias_row, ps[0:1, ROW_BANK, 0:CH], bqv_row[:, 0:CH], ALU.add)
                in_parts(q_parts, bias_row, CH).then_inc(bias_ready, 1)
                with dve.Fori(1, PAIRS // 2) as j:
                    split_x(2 * j, 0)
                    k_sum(2 * j - 1, 1)
                    split_x(2 * j + 1, 1)
                    k_sum(2 * j, 0)
                k_sum(PAIRS - 1, 1)

                dve.wait_ge(kx_done, PAIRS * (i + 1))
                for h in range(HALVES):
                    ins = nc.vector.tensor_copy(kx_sb[:, h, :], ps[:, KX_BANK + h, 0:XO])
                ins.then_inc(fold_in, 1)
                dve.drain()
                nc.vector.tensor_scalar(ksum_eps[:, :], kx_sb[:, :, CH], KSUM_EPS, None, ALU.add)
                dve.drain()
                for h in range(HALVES):
                    nc.vector.tensor_scalar(den_w[:, h, :], densel[:, h, :], ksum_eps[:, h:h + 1], None, ALU.mult)
                dve.wait_ge(fold_mm, 2 * i + 1)
                nc.vector.tensor_copy(ksum_row[:, :], ps[0:1, 0, 0:CH])
                nc.vector.tensor_copy(kxt_sb[:, :, :].rearrange("p h m -> p (h m)"), ps[:, 1, :]).then_inc(fold_in, 1)
                dve.wait_ge(fold_mm, 2 * i + 2)
                for h in range(HALVES):
                    ins = nc.vector.tensor_tensor(kv_w[:, h, :], ps[:, 2, h * P:(h + 1) * P], headmask[:, :], ALU.mult)
                ins.then_inc(fold_in, 1)

                def q_sum(t, par):
                    for h in range(HALVES):
                        dve.wait_ge(ql_ready, 2 * (NB * i + t) + h + 1)
                        nc.vector.scalar_tensor_tensor(q_sb[:, par, h, :], ps[:, QZ_BANK + 2 * par + h, :], 0.0,
                                                       q_act[:, par, h, :], ALU.max, ALU.add).then_inc(q_ready, 1)

                def reciprocals(t):
                    dve.wait_ge(den_mm, NB * i + t + 1)
                    nc.vector.reciprocal(rden, ps[:, DEN_BANK, 0:P])
                    dve.drain()
                    nc.vector.tensor_copy(rden_high, rden)
                    dve.drain()
                    nc.vector.scalar_tensor_tensor(rden_rest, rden_high, partsel[:, 0:1], rden, ALU.mult, ALU.add)
                    dve.drain()
                    nc.vector.tensor_copy(rden_high, rden_rest)
                    dve.drain()
                    nc.vector.scalar_tensor_tensor(rden_parts, rden_high, partsel[:, 1:2], rden_rest,
                                                   ALU.mult, ALU.add).then_inc(rden_ready, 1)

                def output(t):
                    dve.wait_ge(num_mm, NB * i + t + 1)
                    dve.wait_ge(wide_evac, 2 * (NB * i + t + 1))
                    if not first(t, 1):
                        dve.wait_ge(out_ready, NB * i + t)
                    nc.vector.tensor_tensor(ratio[:, :, :], ps[:, NUM_BANK:NUM_BANK + 2, :], rden_wide[:, :, :],
                                            ALU.mult).then_inc(num_read, 1)

                LAG = 4
                q_sum(0, 0)
                reciprocals(0)
                q_sum(1, 1)
                for t in range(1, LAG):
                    output(t - 1)
                    reciprocals(t)
                    q_sum(t + 1, (t + 1) % 2)
                with dve.Fori(LAG // 2, NB // 2 - 1) as j:
                    for t, par in ((2 * j, 0), (2 * j + 1, 1)):
                        output(t - 1)
                        reciprocals(t)
                        q_sum(t + 1, 1 - par)
                        if not last:
                            stat_loaded(i + 1, t - LAG, j - LAG // 2, par)
                for t in (NB - 2, NB - 1):
                    output(t - 1)
                    reciprocals(t)
                    if t == NB - 2:
                        q_sum(NB - 1, 1)
                output(NB - 1)
                if not last:
                    for t in range(NB - 2 - LAG, NB):
                        stat_loaded(i + 1, t, t // 2, t % 2)
                    groupnorm(2 * i + 2)

            images(dve, image)

        @block.tensor
        def _(pe):
            mm = nc.tensor.matmul

            def groupnorm(n):
                pe.wait_ge(gn_in, 3 * n + 1)
                mm(ps[:, GN_BANK, 0:4], gmean[:, :], mean_var[:, :, :].rearrange("p h s -> p (h s)"),
                   start=True, stop=True).then_inc(gn_mm, 1)
                pe.wait_ge(gn_in, 3 * n + 2)
                mm(ps[:, GN_BANK, 4:6], gmean[:, :], gn_dev[:, :], start=True, stop=True).then_inc(gn_mm, 1)

            pe.wait_ge(init_done, 1)
            pe.wait_ge(w_max_in, 1)
            mm(ps[0:1, GN_BANK, 0:P], w_max[:, :], ident[:, :], start=True, stop=True).then_inc(w_max_mm, 1)
            pe.wait_ge(w_max_in, 2)
            mm(ps[:, GN_BANK, 0:2], one_row, w_pow[:, :], start=True, stop=True).then_inc(w_max_mm, 1)
            groupnorm(0)

            def image(i, last):
                def y_of(b, par):
                    pe.wait_ge(xn_ready, NB * i + b + 1)
                    if not first(b, 1):
                        pe.wait_ge(y_evac, NB * i + b)
                    for h in range(HALVES):
                        ins = mm(ps[:, Y_BANK, :].rearrange("p (r c) -> p r c", r=BR), w1_s[:, h, :],
                                 xn[:, par, h, :, 1:1 + COLS], start=(h == 0), stop=(h == HALVES - 1))
                    ins.then_inc(y_mm, 1)

                def fill(b, par, f):
                    if not (first(b, 1) and f < 2):
                        pe.wait_ge(xt_evac, FILLS * (NB * i + b) + f - 1)
                    for c in range(4):
                        n = 4 * f + c
                        r, kw, h = n // 6, n // 2 % 3, n % 2
                        ins = mm(ps[:, XT_BANK + f % 2, c * P:(c + 1) * P], xn[:, par, h, r, kw:kw + COLS], ident[:, :],
                                 start=True, stop=True, is_transpose=True)
                    ins.then_inc(xt_mm, 1)

                def depthwise(b, par):
                    pe.wait_ge(y_halo, NB * i + b + 1)
                    if not first(b, 1):
                        pe.wait_ge(y2_evac, NB * i + b)
                    for k in range(TAPS):
                        kh, kw = divmod(k, KW)
                        ins = mm(ps[:, Y2_BANK, 0:2 * COLS].rearrange("p (r c) -> p r c", r=2), wdiag[:, k, :],
                                 y[:, par, kh:kh + 2, kw:kw + COLS], start=(k == 0), stop=(k == TAPS - 1))
                    ins.then_inc(y2_mm, 1)

                def weights(s, par, r):
                    row = BR * s + r
                    if r == 0:
                        pe.wait_ge(y2_evac, NB * i + s + 1)
                    if not (first(s, 1) and r < 2):
                        pe.wait_ge(mult_done, ROWS * i + row - 1)
                    lo = CR * (r // 2)
                    mm(ps[:, W_BANK + r % 2, 0:NW], ones_bf[:, 0:P], b2_parts[:, :], start=True, stop=False)
                    mm(ps[:, W_BANK + r % 2, 0:NW], y2[lo:lo + CR, par, r % 2, :], w2_s[lo:lo + CR, :],
                       start=False, stop=True).then_inc(w_ready, 1)

                def gather_last(s, par, r):
                    pe.wait_ge(mult_done, ROWS * i + BR * s + r + 1)
                    if not first(s, 1) and r % 2 == 0:
                        pe.wait_ge(x1_done, PAIRS * i + 2 * s + r // 2 - 1)
                    for h in range(HALVES):
                        o = h * 256 + (r % 2) * P
                        ins = mm(ps[:, INV_BANK + r // 2, o:o + P], prod[:, r % 2, TAPS - 1, h * P:(h + 1) * P], ident[:, :],
                                 start=(r % 2 == 0 and h == 0), stop=False, is_transpose=True)
                    ins.then_inc(last_used, 1)

                def gather(s, par, r):
                    pe.wait_ge(sum_done, ROWS * i + BR * s + r + 1)
                    for h in range(HALVES):
                        o = h * 256 + (r % 2) * P
                        for k in range(KW):
                            ins = mm(ps[:, INV_BANK + r // 2, o:o + P], sums[:, r % 2, k, h * P:(h + 1) * P], ident[:, :],
                                     start=False, stop=(r % 2 == 1 and h == 1 and k == KW - 1), is_transpose=True)
                    ins.then_inc(inv_ready, 1)

                def step(s, par):
                    now, before, nxt, nxt2 = ahead(s, 0), ahead(s, -1), ahead(s, 1), ahead(s, 2)
                    if now:
                        weights(s, par, 0)
                        if before:
                            gather_last(s - 1, 1 - par, 2)
                            gather(s - 1, 1 - par, 2)
                    if nxt2:
                        y_of(s + 2, par)
                    if now:
                        weights(s, par, 1)
                        if before:
                            gather_last(s - 1, 1 - par, 3)
                    if nxt:
                        fill(s + 1, 1 - par, 0)
                        fill(s + 1, 1 - par, 1)
                    if now:
                        if before:
                            gather(s - 1, 1 - par, 3)
                        weights(s, par, 2)
                        gather_last(s, par, 0)
                    if nxt:
                        fill(s + 1, 1 - par, 2)
                        fill(s + 1, 1 - par, 3)
                    if now:
                        gather(s, par, 0)
                        weights(s, par, 3)
                        gather_last(s, par, 1)
                    if nxt:
                        fill(s + 1, 1 - par, 4)
                        fill(s + 1, 1 - par, 5)
                        depthwise(s + 1, 1 - par)
                    if now:
                        gather(s, par, 1)

                block_steps(pe, step)
                gather_last(NB - 1, 1, 2)
                gather_last(NB - 1, 1, 3)
                gather(NB - 1, 1, 2)
                gather(NB - 1, 1, 3)
                groupnorm(2 * i + 1)

                def k_of(u, par):
                    pe.wait_ge(xs_ready, PAIRS * i + u + 1)
                    if not first(u, 2):
                        pe.wait_ge(k_ready, PAIRS * i + u - 1)
                    for t in range(2):
                        z = ps[:, KZ_BANK + par, t * CH:(t + 1) * CH]
                        mm(z, ones_bf[:, 0:P], k_parts[:, :], start=True, stop=False)
                        for h in range(HALVES):
                            for xp, wp in ((0, 0), (0, 1), (1, 0)):
                                ins = mm(z, x_parts[:, par, xp, h, t * P:(t + 1) * P], wk_parts[:, wp, h, :],
                                         start=False, stop=(h == 1 and xp == 1))
                    ins.then_inc(kz_mm, 1)
                    if not first(u, 2):
                        pe.wait_ge(kt_evac, PAIRS * i + u - 1)
                    for t in range(2):
                        for h in range(HALVES):
                            o = t * CH + h * P
                            ins = mm(ps[:, KT_BANK + par, o:o + P], xs[:, par, h, t * P:(t + 1) * P], ident[:, :],
                                     start=True, stop=True, is_transpose=True)
                    ins.then_inc(kt_mm, 1)

                def kx_add(u, par):
                    pe.wait_ge(k_ready, PAIRS * i + u + 1)
                    pe.wait_ge(kt_evac, PAIRS * i + u + 1)
                    for t in range(2):
                        for h in range(HALVES):
                            ins = mm(ps[:, KX_BANK + h, 0:XO], k_sb[:, par, t, h * P:(h + 1) * P], xt_sb[:, par, t, :],
                                     start=(first(u, 1) and t == 0), stop=(isinstance(u, int) and u == PAIRS - 1 and t == 1))
                    ins.then_inc(kx_done, 1)

                k_of(0, 0)
                k_of(1, 1)
                pe.wait_ge(w_scaled, i + 1)
                for h in range(HALVES):
                    ins = mm(ps[0:1, ROW_BANK, 0:CH], gn_neg[:, h:h + 1], wqv[:, h, 0:CH],
                             start=(h == 0), stop=(h == HALVES - 1))
                ins.then_inc(row_mm, 1)
                kx_add(0, 0)
                with pe.Fori(1, PAIRS // 2) as j:
                    k_of(2 * j, 0)
                    kx_add(2 * j - 1, 1)
                    k_of(2 * j + 1, 1)
                    kx_add(2 * j, 0)
                kx_add(PAIRS - 1, 1)

                pe.wait_ge(fold_in, 3 * i + 1)
                for h in range(HALVES):
                    mm(ps[0:1, 0, h * P:(h + 1) * P], kx_sb[:, h, CH:XO], ident[:, :], start=True, stop=True)
                for ih in range(HALVES):
                    for h in range(HALVES):
                        o = ih * CH + h * P
                        ins = mm(ps[:, 1, o:o + P], kx_sb[:, h, ih * P:(ih + 1) * P], ident[:, :],
                                 start=True, stop=True, is_transpose=True)
                ins.then_inc(fold_mm, 1)
                pe.wait_ge(fold_in, 3 * i + 2)
                for h in range(HALVES):
                    kv = ps[:, 2, h * P:(h + 1) * P]
                    for ih in range(HALVES):
                        mm(kv, kxt_sb[:, ih, h * P:(h + 1) * P], wqv[:, ih, CH + h * P:CH + (h + 1) * P],
                           start=(ih == 0), stop=False)
                    ins = mm(kv, ksum_row[:, h * P:(h + 1) * P], bqv_row[:, CH + h * P:CH + (h + 1) * P],
                             start=False, stop=True)
                ins.then_inc(fold_mm, 1)

                pe.wait_ge(fold_in, 3 * i + 3)
                pe.wait_ge(bias_ready, i + 1)

                def q_of(t, par, h):
                    if not first(t, 2):
                        pe.wait_ge(q_ready, 2 * (NB * i + t) + h - 3)
                    z = ps[:, QZ_BANK + 2 * par + h, :]
                    mm(z, q_parts[:, h * P:(h + 1) * P], ones_bf[:, :], start=True, stop=False)
                    for ih in range(HALVES):
                        ins = mm(z, wqv[:, ih, h * P:(h + 1) * P], X[:, ih, bass.ds(t * BP, BP)], start=False, stop=(ih == 1))
                    ins.then_inc(qz_mm, 1)

                def denominators(t, par):
                    pe.wait_ge(q_ready, 2 * (NB * i + t) + 2)
                    if not first(t, 1):
                        pe.wait_ge(wide_evac, 2 * (NB * i + t))
                    for h in range(HALVES):
                        for c in range(BR):
                            ins = mm(ps[32 * c:32 * c + DEN_COLS, DEN_BANK, 0:P], den_w[:, h, :],
                                     q_sb[:, par, h, c * P:(c + 1) * P], start=(h == 0), stop=(h == 1),
                                     tile_position=(0, 32 * c))
                    ins.then_inc(den_mm, 1)

                def numerators(t, par):
                    if not first(t, 1):
                        pe.wait_ge(num_read, NB * i + t)
                    for h in range(HALVES):
                        ins = mm(ps[:, NUM_BANK + h, :], kv_w[:, h, :], q_sb[:, par, h, :], start=True, stop=True)
                    ins.then_inc(num_mm, 1)

                def widen(t):
                    pe.wait_ge(rden_ready, NB * i + t + 1)
                    for h in range(HALVES):
                        for c in range(BR):
                            ins = mm(ps[:, WIDE_BANK[h], c * P:(c + 1) * P], headsel[:, c, h, :], rden_parts[:, :],
                                     start=True, stop=True)
                        ins.then_inc(wide_mm, 1)

                def c_step(t, par, more):
                    if more:
                        q_of(t + 1, 1 - par, 0)
                    denominators(t, par)
                    if more:
                        q_of(t + 1, 1 - par, 1)
                    numerators(t, par)
                    widen(t)

                pe.wait_ge(sel_loaded, 16 * (i + 1))
                q_of(0, 0, 0)
                q_of(0, 0, 1)
                c_step(0, 0, True)
                c_step(1, 1, True)
                with pe.Fori(1, NB // 2 - 1) as j:
                    c_step(2 * j, 0, True)
                    c_step(2 * j + 1, 1, True)
                c_step(NB - 2, 0, True)
                c_step(NB - 1, 1, False)
                if not last:
                    groupnorm(2 * i + 2)

            images(pe, image)


_OUT = "out_dram"


def kernel(**inputs):
    import numpy as np
    import concourse.bacc as bacc
    from concourse.bass_utils import run_bass_kernel_spmd

    a = {k: np.asarray(v) for k, v in inputs.items()}
    w1t = a["L0_conv_w1"].T
    w2t = a["L0_conv_w2"].reshape(GROUPS, TAPS, CR).transpose(2, 1, 0).reshape(CR, NW)
    arrays = {
        "x": a["x"],
        "w1t": np.concatenate([w1t, w1t], axis=1),
        "b1": np.concatenate([a["L0_conv_b1"]] * 2).reshape(P, 1),
        "wd": np.concatenate([a["L0_conv_wd"].reshape(CR, TAPS)] * 2),
        "bd": np.concatenate([a["L0_conv_bd"]] * 2).reshape(P, 1),
        "w2t": np.concatenate([w2t, w2t]),
        "b2": a["L0_conv_b2"].reshape(GROUPS, TAPS).T.reshape(1, NW),
        "wk": a["L1_conv_Wk"].T,
        "bk": a["L1_conv_bk"].reshape(1, CH),
        "wqv": np.concatenate([a["L1_conv_Wq"].T, a["L1_conv_Wv"].T], axis=1),
        "bqv": np.concatenate([a["L1_conv_bq"], a["L1_conv_bv"]]).reshape(1, 2 * CH),
    }
    c = np.arange(P)
    head = c[:, None] // 32 + 4 * np.arange(HALVES)[None, :]
    sel = (head[:, :, None] == (np.arange(DEN_COLS) % HEADS)[None, None, :]).astype(np.float32)
    once = (sel * (np.arange(DEN_COLS) < PARTS * HEADS)).transpose(2, 1, 0)[:, None]
    part = (c % DEN_COLS) // HEADS
    arrays.update({
        "ident": np.eye(P, dtype=np.float32),
        "gmean": ((c[:, None] // 8 == c[None, :] // 8) / 8.0).astype(np.float32),
        "headmask": (c[:, None] // 32 == c[None, :] // 32).astype(np.float32),
        "densel": sel,
        "partsel": -(part[:, None] > np.arange(PARTS - 1)[None, :]).astype(np.float32),
        "headsel": np.concatenate([once * (np.arange(BR) == q)[None, :, None, None] for q in range(BR)]).astype(mybir.dt.np(BF16)),
    })
    arrays = {f"{k}_in": np.ascontiguousarray(v) for k, v in arrays.items()}
    nc = bacc.Bacc("TRN2", target_bir_lowering=False, num_devices=1)
    args = [nc.dram_tensor(k, v.shape, mybir.dt.from_np(v.dtype), kind="ExternalInput").ap() for k, v in arrays.items()]
    args.append(nc.dram_tensor(_OUT, (IMAGES, CH, ROWS, COLS), F32, kind="ExternalOutput").ap())
    two_block_kernel(nc, *args)
    r = run_bass_kernel_spmd(nc, [arrays], core_ids=[0])
    return r.results[0][_OUT]
```

```python
from contextlib import ExitStack

import concourse.bass as bass
from concourse import mybir

F32 = mybir.dt.float32
BF16 = mybir.dt.bfloat16
FP16 = mybir.dt.float16
I32 = mybir.dt.int32
ALU = mybir.AluOpType
ACT = mybir.ActivationFunctionType

P = 128
IMAGES, CH, ROWS, COLS = 8, 256, 128, 128
HALVES = CH // P
PIX = ROWS * COLS
TAPS = 9
KW = 3
GROUPS = 16
GC = CH // GROUPS
CR = 64
NW = TAPS * GROUPS
BR = 4
NB = ROWS // BR
TAIL = 3
LOADS = ((NB - TAIL + 1) // 2, (NB - TAIL) // 2)
BP = BR * COLS
PADW = COLS + 2
RING = 8
ROWT = KW * CH
FILLS = BR * HALVES // 4
PAIRS = ROWS // 2
HEADS = 8
GN_EPS = 1e-5
KSUM_EPS = 1e-6
EXPONENT = 0x7F800000
W_TINY = 1e-6
W_RANGE = 512.0
BIAS_ROWS = 96
PARTS = 3
DEN_COLS = 32


def two_block_kernel(nc, x, w1t, b1, wd, bd, w2t, b2, wk, bk, wqv_in, bq, bv,
                     ident_in, gmean_in, headmask_in, densel_in, partsel_in, headsel_in, out):
    x_v = x.rearrange("b (h p) r c -> b p h (r c)", p=P)
    out_v = out.rearrange("b (h p) r c -> b p h (r c)", p=P)

    with ExitStack() as ctx:
        def sb(name, shape, dt=F32):
            return ctx.enter_context(nc.sbuf_tensor(name, shape, dt))

        def sem(name):
            return ctx.enter_context(nc.semaphore(name))

        X = sb("X", [P, HALVES, PIX])
        w1_s = sb("w1_s", [P, HALVES, P])
        b1_s = sb("b1_s", [P, 1])
        wd_s = sb("wd_s", [P, TAPS])
        wdiag = sb("wdiag", [P, TAPS, P])
        zero_row = sb("zero_row", [P, PADW])
        bd_s = sb("bd_s", [P, 1])
        w2_s = sb("w2_s", [P, NW])
        wk_parts = sb("wk_parts", [P, 2, HALVES, CH], FP16)
        wk_scale = sb("wk_scale", [P, 2])
        bv_row = sb("bv_row", [1, CH])
        ident = sb("ident", [P, P])
        gmean = sb("gmean", [P, P])
        headmask = sb("headmask", [P, P])
        densel = sb("densel", [P, HALVES, DEN_COLS])
        partsel = sb("partsel", [P, 2])
        ones_bf = sb("ones_bf", [BIAS_ROWS, P], BF16)
        b2_parts = sb("b2_parts", [BIAS_ROWS, NW], BF16)
        k_parts = sb("k_parts", [BIAS_ROWS, CH], BF16)
        bq_s = sb("bq_s", [P, HALVES])
        q_bias = sb("q_bias", [P, HALVES])

        stats = sb("stats", [P, HALVES, NB, 6])
        mean_var = sb("mean_var", [P, HALVES, 2])
        gn_mean = sb("gn_mean", [P, 2])
        gn_avg = sb("gn_avg", [P, 2])
        gn_dev = sb("gn_dev", [P, 2])
        gn_var = sb("gn_var", [P, 2])
        gn_ln = sb("gn_ln", [P, 2])
        gn_r0 = sb("gn_r0", [P, 2])
        gn_t = sb("gn_t", [P, 2])
        gn_rstd = sb("gn_rstd", [P, 2])
        gn_shift = sb("gn_shift", [P, 2])
        gn_neg = sb("gn_neg", [P, 2])

        xn = sb("xn", [P, 2, HALVES, BP])
        w_last = sb("w_last", [P, 2, GROUPS])
        y = sb("y", [P, 2, BR, PADW])
        y_last = sb("y_last", [CR, COLS])
        y2 = sb("y2", [P, 2, 2, COLS])
        place = sb("place", [P, 2 * KW * CH])
        sums = place[:, :].rearrange("p (s k c) -> p s k c", s=2, k=KW)
        wqv = place[:, 0:HALVES * 2 * CH].rearrange("p (h m) -> p h m", h=HALVES)
        arena = sb("arena", [P, RING * ROWT + 2 * TAPS * CH])
        xt = arena[:, 0:RING * ROWT]
        ring = xt.rearrange("p (r k c) -> p r k c", r=RING, k=KW)
        prod = arena[:, RING * ROWT:].rearrange("p (s k c) -> p s k c", s=2, k=TAPS)

        at = [0]

        def piece(n):
            at[0] += n
            return arena[:, at[0] - n:at[0]]

        xs = piece(2 * HALVES * 2 * P).rearrange("p (s h n) -> p s h n", s=2, h=HALVES)
        k_act = piece(2 * 2 * CH).rearrange("p (s n) -> p s n", s=2)
        k_sb = piece(2 * 2 * CH).rearrange("p (s t m) -> p s t m", s=2, t=2)
        XO = CH + 1
        xt_sb = piece(2 * 2 * XO).rearrange("p (s t m) -> p s t m", s=2, t=2)
        kx_sb = piece(HALVES * XO).rearrange("p (h m) -> p h m", h=HALVES)
        kxt_sb = piece(HALVES * CH).rearrange("p (h m) -> p h m", h=HALVES)
        x_parts = piece(2 * 2 * HALVES * 2 * P // 2).bitcast(FP16).rearrange("p (s n h m) -> p s n h m", s=2, n=2, h=HALVES)
        wk_raw = piece(HALVES * CH).rearrange("p (h m) -> p h m", h=HALVES)
        one_row = piece(P)[0:1, :]
        bk_row = piece(CH)[0:1, :]
        ksum_row = piece(CH)[0:1, :]
        b2_row = piece(NW)[0:1, :]
        part_rest = piece(CH)[0:1, :]
        part_mid = piece(CH)[0:1, :].bitcast(BF16)[:, 0:CH]
        fold_end = at[0]
        at[0] = RING * ROWT + 2 * TAPS * CH - HALVES * (P + DEN_COLS) - BR * HALVES * P // 2
        fold_start = at[0]
        assert fold_end <= fold_start
        kv_w = piece(HALVES * P).rearrange("p (h n) -> p h n", h=HALVES)
        den_w = piece(HALVES * DEN_COLS).rearrange("p (h n) -> p h n", h=HALVES)
        headsel = piece(BR * HALVES * P // 2).bitcast(BF16).rearrange("p (c h n) -> p c h n", c=BR, h=HALVES)
        assert at[0] <= RING * ROWT + 2 * TAPS * CH
        at[0] = 0
        q_act = piece(2 * HALVES * BP).rearrange("p (s h n) -> p s h n", s=2, h=HALVES)
        q_sb = piece(2 * HALVES * BP).rearrange("p (s h n) -> p s h n", s=2, h=HALVES)
        rden_wide = piece(HALVES * BP).rearrange("p (h n) -> p h n", h=HALVES)
        ratio = piece(HALVES * BP).rearrange("p (h n) -> p h n", h=HALVES)
        rden = piece(P)
        rden_rest = piece(P)
        rden_high = piece(P // 2).bitcast(BF16)
        rden_parts = piece(P // 2).bitcast(BF16)
        tail = piece(TAIL * HALVES * BP).rearrange("p (t h n) -> p t h n", t=TAIL, h=HALVES)
        assert at[0] <= fold_start

        ksum_eps = sb("ksum_eps", [P, HALVES])
        w_max = sb("w_max", [P, 1])
        w_pow = sb("w_pow", [1, 2])

        ps = ctx.enter_context(nc.psum_tensor("ps", [P, 8, 512], F32))
        XT_BANK, W_BANK, INV_BANK = 0, 4, 6
        Y_BANK, Y2_BANK = 2, 3
        KZ_BANK, KT_BANK, KX_BANK = 0, 2, 4
        QZ_BANK, NUM_BANK, DEN_BANK, WIDE_BANK = 0, 4, 6, (7, 6)
        GN_BANK, SHIFT_BANK = 2, 6
        FOLD_BANK = 6

        const_loaded = sem("const_loaded")
        sel_loaded = sem("sel_loaded")
        w_loaded = sem("w_loaded")
        x_loaded = [sem("x_loaded0"), sem("x_loaded1")]
        tail_loaded = sem("tail_loaded")
        x_placed = sem("x_placed")
        out_stored = [sem("out_stored0"), sem("out_stored1")]
        init_done = sem("init_done")
        gn_in = sem("gn_in")
        gn_mm = sem("gn_mm")
        gn_root = sem("gn_root")
        gn_ready = sem("gn_ready")
        xn_ready = sem("xn_ready")
        y_mm = sem("y_mm")
        y_halo = sem("y_halo")
        y_evac = sem("y_evac")
        y2_mm = sem("y2_mm")
        y2_evac = sem("y2_evac")
        xt_mm = sem("xt_mm")
        xt_evac = sem("xt_evac")
        ring_clear = sem("ring_clear")
        x_shifted = [[sem("x_shifted00"), sem("x_shifted01")], [sem("x_shifted10"), sem("x_shifted11")]]
        w_ready = sem("w_ready")
        w_last_ready = sem("w_last_ready")
        last_made = sem("last_made")
        mult_two = sem("mult_two")
        mult_done = sem("mult_done")
        sum_two = sem("sum_two")
        sum_done = sem("sum_done")
        last_used = sem("last_used")
        inv_ready = sem("inv_ready")
        x1_done = sem("x1_done")
        w_max_in = sem("w_max_in")
        w_max_mm = sem("w_max_mm")
        w_scaled = sem("w_scaled")
        shift_mm = sem("shift_mm")
        bias_ready = sem("bias_ready")
        xs_ready = sem("xs_ready")
        kz_mm = sem("kz_mm")
        kt_mm = sem("kt_mm")
        kl_ready = sem("kl_ready")
        kt_evac = sem("kt_evac")
        k_ready = sem("k_ready")
        kx_done = sem("kx_done")
        fold_in = sem("fold_in")
        fold_mm = sem("fold_mm")
        qz_mm = sem("qz_mm")
        ql_ready = sem("ql_ready")
        qz_read = sem("qz_read")
        q_relu_ready = sem("q_relu_ready")
        q_ready = sem("q_ready")
        den_mm = sem("den_mm")
        rden_ready = sem("rden_ready")
        num_mm = sem("num_mm")
        wide_mm = sem("wide_mm")
        wide_evac = sem("wide_evac")
        num_read = sem("num_read")
        out_ready = sem("out_ready")

        N_CONST = 15
        block = ctx.enter_context(nc.Block())

        def images(eng, image):
            with eng.Fori(0, IMAGES - 1) as i:
                image(i, False)
            image(IMAGES - 1, True)

        def block_steps(eng, step):
            for s in range(-2, 2):
                step(s, s % 2)
            with eng.Fori(1, NB // 2 - 2) as j:
                step(2 * j, 0)
                step(2 * j + 1, 1)
            for s in range(NB - 4, NB):
                step(s, s % 2)

        def ahead(s, n):
            return not isinstance(s, int) or 0 <= s + n < NB

        def moves(i, b, par):
            return 16 * (NB * i + b) + 32 - 16 * par

        def first(s, n):
            return isinstance(s, int) and s < n

        @block.sync
        def _(sp):
            for dst, src in ((w1_s[:, :, :], w1t.rearrange("(h p) n -> p h n", p=P)), (b1_s[:, :], b1), (wd_s[:, :], wd),
                             (bd_s[:, :], bd), (w2_s[:, :], w2t), (b2_row[:, :], b2),
                             (bq_s[:, :], bq), (bv_row[:, :], bv), (wk_raw, wk.rearrange("(h p) n -> p h n", p=P)), (bk_row, bk),
                             (ident[:, :], ident_in), (gmean[:, :], gmean_in), (headmask[:, :], headmask_in),
                             (densel[:, :, :], densel_in), (partsel[:, :], partsel_in)):
                sp.dma_start(dst, src).then_inc(const_loaded, 16)

            def load(i, t, par):
                sp.dma_start(X[:, :, bass.ds(t * BP, BP)], x_v[i, :, :, bass.ds(t * BP, BP)]).then_inc(x_loaded[par], 16)

            load(0, 0, 0)
            load(0, 1, 1)
            with sp.Fori(1, LOADS[1]) as j:
                sp.wait_ge(x_loaded[0], 16 * j)
                load(0, 2 * j, 0)
                sp.wait_ge(x_loaded[1], 16 * j)
                load(0, 2 * j + 1, 1)
            sp.wait_ge(x_loaded[0], 16 * LOADS[1])
            load(0, NB - TAIL - 1, 0)
            for t in range(NB - TAIL, NB):
                sp.dma_start(X[:, :, bass.ds(t * BP, BP)], x_v[0, :, :, bass.ds(t * BP, BP)]).then_inc(x_placed, 16)

            def image(i, last):
                def store(t, par):
                    sp.wait_ge(out_ready, NB * i + t + 1)
                    sp.dma_start(out_v[i, :, :, bass.ds(t * BP, BP)], X[:, :, bass.ds(t * BP, BP)]).then_inc(out_stored[par], 16)

                def next_load(t_half, par):
                    if not last:
                        sp.wait_ge(out_stored[par], 16 * (NB // 2 * i + t_half + 1))
                        sp.wait_ge(x_loaded[par], 16 * (LOADS[par] * (i + 1) + t_half))
                        load(i + 1, 2 * t_half + par, par)

                def shift(b, par, f):
                    sp.wait_ge(xt_evac, FILLS * (NB * i + b) + f + 1)
                    rows = ring[:, par * BR + 2 * f:par * BR + 2 * f + 2, :, :]
                    sp.dma_start(rows[1:P, :, 0, :], rows[0:P - 1, :, 1, :]).then_inc(x_shifted[par][f], 16)
                    sp.dma_start(rows[0:P - 1, :, 2, :], rows[1:P, :, 1, :]).then_inc(x_shifted[par][f], 16)

                sp.wait_ge(ring_clear, i + 1)
                for b in range(2):
                    for f in range(FILLS):
                        shift(b, b, f)
                with sp.Fori(1, NB // 2) as j:
                    for par in range(2):
                        for f in range(FILLS):
                            shift(2 * j + par, par, f)
                sp.wait_ge(x1_done, PAIRS * (i + 1))
                sp.dma_start(wqv, wqv_in.rearrange("(h p) n -> p h n", p=P)).then_inc(w_loaded, 16)
                sp.wait_ge(gn_ready, 2 * i + 2)
                sp.dma_start(headsel, headsel_in).then_inc(sel_loaded, 16)
                store(0, 0)
                store(1, 1)
                next_load(0, 0)
                with sp.Fori(1, LOADS[1]) as j:
                    store(2 * j, 0)
                    next_load(j - 1, 1)
                    store(2 * j + 1, 1)
                    next_load(j, 0)
                store(NB - TAIL - 1, 0)
                next_load(LOADS[1] - 1, 1)
                store(NB - TAIL, 1)
                next_load(LOADS[0] - 1, 0)

                def place_tail(t):
                    if not last:
                        sp.wait_ge(out_stored[t % 2], 16 * (NB // 2 * i + t // 2 + 1))
                        sp.dma_start(X[:, :, t * BP:(t + 1) * BP], tail[:, t - (NB - TAIL), :, :]).then_inc(x_placed, 16)

                store(NB - 2, 0)
                if not last:
                    sp.wait_ge(tail_loaded, 16 * TAIL * (i + 1))
                place_tail(NB - 3)
                store(NB - 1, 1)
                place_tail(NB - 2)
                place_tail(NB - 1)

            images(sp, image)
            for par in range(2):
                sp.wait_ge(out_stored[par], 16 * (NB // 2) * IMAGES)

        @block.gpsimd
        def _(pool):
            def image(i, last):
                def add_products(s, par, r):
                    row = BR * s + r
                    pool.wait_ge(mult_two, ROWS * i + row + 1)
                    if not (first(s, 1) and r < 2):
                        pool.wait_ge(inv_ready, ROWS * i + row - 1)
                    nc.gpsimd.tensor_tensor(sums[:, r % 2, :, :], prod[:, r % 2, 0:KW, :], prod[:, r % 2, KW:2 * KW, :],
                                            ALU.add).then_inc(sum_two, 1)
                    pool.wait_ge(w_last_ready, ROWS * i + row + 1)
                    if not (first(s, 1) and r < 2):
                        pool.wait_ge(last_used, ROWS * i + row - 1)
                    if r % 2 == 1 and not (isinstance(s, int) and s == NB - 1 and r == BR - 1):
                        nb, npar = (s, par) if r == 1 else (s + 1, 1 - par)
                        pool.wait_ge(x_shifted[npar][1 - r // 2], moves(i, nb, npar))
                    if first(s, 1) and r == 0:
                        pool.wait_ge(x_shifted[0][0], moves(i, 0, 0))
                    slot = (BR * par + r + 1) % RING
                    nc.gpsimd.tensor_tensor(
                        prod[:, r % 2, TAPS - 1, :].rearrange("p (g c) -> p g c", c=GC),
                        w_last[:, r % 2, :].unsqueeze(2).to_broadcast([P, GROUPS, GC]),
                        ring[:, slot, KW - 1, :].rearrange("p (g c) -> p g c", c=GC), ALU.mult).then_inc(last_made, 1)
                    pool.wait_ge(mult_done, ROWS * i + row + 1)
                    pool.wait_ge(sum_two, ROWS * i + row + 1)
                    nc.gpsimd.tensor_tensor(sums[:, r % 2, 0, :], sums[:, r % 2, 0, :], prod[:, r % 2, 2 * KW, :],
                                            ALU.add).then_inc(sum_done, 1)

                def add_block(s, par):
                    for r in range(BR):
                        add_products(s, par, r)

                add_block(0, 0)
                add_block(1, 1)
                with pool.Fori(1, NB // 2 - 1) as j:
                    add_block(2 * j, 0)
                    add_block(2 * j + 1, 1)
                add_block(NB - 2, 0)
                add_block(NB - 1, 1)

                def add_output(t):
                    xa = X[:, :, bass.ds(t * BP, BP)]
                    pool.wait_ge(num_read, NB * i + t + 1)
                    nc.gpsimd.tensor_tensor(xa, ratio[:, :, :], xa, ALU.add).then_inc(out_ready, 1)

                def q_sum(t, par):
                    for h in range(HALVES):
                        pool.wait_ge(q_relu_ready, 2 * (NB * i + t) + h + 1)
                        pool.wait_ge(ql_ready, 2 * (NB * i + t) + h + 1)
                        nc.gpsimd.tensor_tensor(q_sb[:, par, h, :], q_sb[:, par, h, :], q_act[:, par, h, :],
                                                ALU.add).then_inc(q_ready, 1)

                q_sum(0, 0)
                q_sum(1, 1)
                with pool.Fori(1, NB // 2) as j:
                    add_output(2 * j - 2)
                    q_sum(2 * j, 0)
                    add_output(2 * j - 1)
                    q_sum(2 * j + 1, 1)
                add_output(NB - 2)
                add_output(NB - 1)

            images(pool, image)

        @block.scalar
        def _(act):
            def gn_guess(n):
                act.wait_ge(gn_in, 3 * n + 3)
                nc.scalar.activation(gn_ln[:, :], gn_var[:, :], ACT.Ln)
                act.drain()
                nc.scalar.activation(gn_r0[:, :], gn_ln[:, :], ACT.Exp, scale=-0.5).then_inc(gn_root, 1)

            def normalise(i, b, par):
                if not first(b, 2):
                    act.wait_ge(xt_mm, FILLS * (NB * i + b - 1))
                for h in range(HALVES):
                    ins = nc.scalar.activation(
                        xn[:, par, h, :], X[:, h, bass.ds(b * BP, BP)],
                        ACT.Identity, bias=gn_shift[:, h:h + 1], scale=gn_rstd[:, h:h + 1])
                ins.then_inc(xn_ready, 1)

            def y_out(i, b, par):
                act.wait_ge(y_mm, NB * i + b + 1)
                yp = ps[:, Y_BANK, :].rearrange("p (r c) -> p r c", r=BR)

                def put(lo, dst, src):
                    return nc.scalar.activation(dst, src, ACT.Identity, bias=b1_s[lo:lo + CR, :])

                if first(b, 1):
                    nc.scalar.copy(y[0:CR, par, 0, :], zero_row[0:CR, :])
                else:
                    put(CR, y[CR:P, 1 - par, BR - 1:BR, 1:1 + COLS], yp[CR:P, 0:1, :]).then_inc(y_halo, 1)
                    nc.scalar.copy(y[0:CR, par, 0, 1:1 + COLS], y_last[:, :])
                put(0, y[0:CR, par, 1:BR, 1:1 + COLS], yp[0:CR, 0:BR - 1, :])
                put(CR, y[CR:P, par, 0:BR - 1, 1:1 + COLS], yp[CR:P, 1:BR, :])
                if not (isinstance(b, int) and b == 0):
                    act.drain()
                put(0, y_last[:, :], yp[0:CR, BR - 1, :]).then_inc(y_evac, 1)
                if isinstance(b, int) and b == NB - 1:
                    nc.scalar.copy(y[CR:P, par, BR - 1, :], zero_row[CR:P, :]).then_inc(y_halo, 1)

            def y2_out(i, b, par):
                act.wait_ge(y2_mm, NB * i + b + 1)
                nc.scalar.activation(y2[:, par, :, :], ps[:, Y2_BANK, 0:2 * COLS].rearrange("p (r c) -> p r c", r=2),
                                     ACT.Identity, bias=bd_s[:, :]).then_inc(y2_evac, 1)

            def xt_out(i, b, par):
                for f in range(FILLS):
                    if not first(b, 2):
                        act.wait_ge(mult_done, ROWS * i + BR * b - 5 + 2 * f)
                    act.wait_ge(xt_mm, FILLS * (NB * i + b) + f + 1)
                    r = par * BR + 2 * f
                    nc.scalar.copy(ring[:, r:r + 2, 1, :], ps[:, XT_BANK + f, :].rearrange("p (r c) -> p r c", r=2)
                                   ).then_inc(xt_evac, 1)

            def softplus_log(dst, z, scale=1.0, bias=0.0, z_read=None):
                ins = nc.scalar.activation(dst, z, ACT.Abs, scale=scale, bias=bias)
                if z_read is not None:
                    ins.then_inc(z_read, 1)
                act.drain()
                nc.scalar.activation(dst, dst, ACT.Exp, scale=-1.0)
                act.drain()
                return nc.scalar.activation(dst, dst, ACT.Ln, bias=1.0)

            nc.scalar.preload_act_table_set("natural_log_exp_and_others")
            act.wait_ge(init_done, 1)
            gn_guess(0)

            def image(i, last):
                act.wait_ge(gn_ready, 2 * i + 1)
                normalise(i, 0, 0)
                normalise(i, 1, 1)

                def step(s, par):
                    if isinstance(s, int) and s == 1:
                        act.wait_ge(x_placed, 16 * TAIL * (i + 1))
                    starts = isinstance(s, int) and s < 0
                    if ahead(s, 2):
                        y_out(i, s + 2, par)
                    if isinstance(s, int) and s == -2:
                        xt_out(i, 0, 0)
                    if ahead(s, 1):
                        if not starts:
                            xt_out(i, s + 1, 1 - par)
                        y2_out(i, s + 1, 1 - par)
                    if ahead(s, 3) and not (isinstance(s, int) and s == -2):
                        normalise(i, s + 3, 1 - par)

                block_steps(act, step)
                gn_guess(2 * i + 1)

                def k_pair(u, par):
                    act.wait_ge(kz_mm, PAIRS * i + u + 1)
                    if not first(u, 2):
                        act.wait_ge(k_ready, PAIRS * i + u - 1)
                    softplus_log(k_act[:, par, :], ps[:, KZ_BANK + par, :], wk_scale[:, 1:2]).then_inc(kl_ready, 1)
                    act.wait_ge(kt_mm, PAIRS * i + u + 1)
                    if not first(u, 2):
                        act.wait_ge(kx_done, PAIRS * i + u - 1)
                    nc.scalar.copy(xt_sb[:, par, :, 0:CH], ps[:, KT_BANK + par, :].rearrange("p (t m) -> p t m", t=2)
                                   ).then_inc(kt_evac, 1)

                k_pair(0, 0)
                k_pair(1, 1)
                with act.Fori(1, PAIRS // 2) as j:
                    k_pair(2 * j, 0)
                    k_pair(2 * j + 1, 1)

                def q_log(t, par):
                    for h in range(HALVES):
                        act.wait_ge(qz_mm, 2 * (NB * i + t) + h + 1)
                        softplus_log(q_act[:, par, h, :], ps[:, QZ_BANK + 2 * par + h, :],
                                     bias=q_bias[:, h:h + 1], z_read=qz_read).then_inc(ql_ready, 1)

                def wide_out(t):
                    for h in range(HALVES):
                        act.wait_ge(wide_mm, 2 * (NB * i + t) + h + 1)
                        if h == 0 and not first(t, 1):
                            act.wait_ge(num_read, NB * i + t)
                        nc.scalar.copy(rden_wide[:, h, :], ps[:, WIDE_BANK[h], :]).then_inc(wide_evac, 1)

                act.wait_ge(bias_ready, i + 1)
                q_log(0, 0)
                if not last:
                    act.wait_ge(fold_in, 3 * i + 3)
                    for k in range(TAIL):
                        t = NB - TAIL + k
                        act.dma_start(tail[:, k, :, :], x_v[i + 1, :, :, t * BP:(t + 1) * BP]).then_inc(tail_loaded, 16)
                q_log(1, 1)
                wide_out(0)
                with act.Fori(1, NB // 2) as j:
                    q_log(2 * j, 0)
                    wide_out(2 * j - 1)
                    q_log(2 * j + 1, 1)
                    wide_out(2 * j)
                wide_out(NB - 1)
                if not last:
                    gn_guess(2 * i + 2)

            images(act, image)

        @block.vector
        def _(dve):
            def stat(t):
                for h in range(HALVES):
                    nc.vector.bn_stats(stats[:, h, bass.ds(t, 1), :], X[:, h, bass.ds(t * BP, BP)])

            def stat_loaded(n, t, t_half, par):
                dve.wait_ge(x_loaded[par], 16 * (LOADS[par] * n + t_half + 1))
                stat(t)

            def groupnorm_start():
                dve.drain()
                for h in range(HALVES):
                    ins = nc.vector.bn_aggr(mean_var[:, h, :], stats[:, h, :, :].rearrange("p t s -> p (t s)"))
                ins.then_inc(gn_in, 1)

            def groupnorm_end(n, meanwhile=None):
                dve.wait_ge(gn_mm, 2 * n + 1)
                means = ps[:, GN_BANK, 0:4].rearrange("p (h s) -> p h s", h=2)
                nc.vector.tensor_copy(gn_mean[:, :], means[:, :, 0])
                nc.vector.tensor_copy(gn_avg[:, :], means[:, :, 1])
                dve.drain()
                nc.vector.tensor_tensor(gn_dev[:, :], mean_var[:, :, 0], gn_mean[:, :], ALU.subtract)
                dve.drain()
                nc.vector.tensor_tensor(gn_dev[:, :], gn_dev[:, :], gn_dev[:, :], ALU.mult).then_inc(gn_in, 1)
                dve.wait_ge(gn_mm, 2 * n + 2)
                nc.vector.scalar_tensor_tensor(gn_var[:, :], ps[:, GN_BANK, 4:6], GN_EPS, gn_avg[:, :],
                                               ALU.add, ALU.add).then_inc(gn_in, 1)
                if meanwhile is not None:
                    meanwhile()
                dve.wait_ge(gn_root, n + 1)
                nc.vector.tensor_tensor(gn_t[:, :], gn_r0[:, :], gn_r0[:, :], ALU.mult)
                dve.drain()
                nc.vector.tensor_tensor(gn_t[:, :], gn_t[:, :], gn_var[:, :], ALU.mult)
                dve.drain()
                nc.vector.tensor_scalar(gn_t[:, :], gn_t[:, :], -0.5, 1.5, ALU.mult, ALU.add)
                dve.drain()
                nc.vector.tensor_tensor(gn_rstd[:, :], gn_r0[:, :], gn_t[:, :], ALU.mult)
                dve.drain()
                nc.vector.tensor_scalar(gn_neg[:, :], gn_mean[:, :], -1.0, None, ALU.mult)
                nc.vector.scalar_tensor_tensor(gn_shift[:, :], gn_mean[:, :], -1.0, gn_rstd[:, :],
                                               ALU.mult, ALU.mult).then_inc(gn_ready, 1)

            def in_parts(parts, row, n):
                dve.drain()
                nc.vector.tensor_copy(parts[0:1, 0:n], row)
                dve.drain()
                nc.vector.tensor_tensor(part_rest[:, 0:n], row, parts[0:1, 0:n], ALU.subtract)
                dve.drain()
                nc.vector.tensor_copy(part_mid[:, 0:n], part_rest[:, 0:n])
                dve.drain()
                nc.vector.tensor_copy(parts[32:33, 0:n], part_mid[:, 0:n])
                nc.vector.tensor_tensor(part_rest[:, 0:n], part_rest[:, 0:n], part_mid[:, 0:n], ALU.subtract)
                dve.drain()
                return nc.vector.tensor_copy(parts[64:65, 0:n], part_rest[:, 0:n])

            nc.vector.memset(y[:, :, :, :], 0.0)
            nc.vector.memset(b2_parts[:, :], 0.0)
            nc.vector.memset(k_parts[:, :], 0.0)
            nc.vector.memset(one_row, 1.0)
            nc.vector.memset(ones_bf[:, :], 1.0)
            nc.vector.memset(zero_row[:, :], 0.0)
            dve.wait_ge(const_loaded, 16 * N_CONST)
            for k in range(TAPS):
                nc.vector.tensor_scalar(wdiag[:, k, :], ident[:, :], wd_s[:, k:k + 1], None, ALU.mult)
            in_parts(b2_parts, b2_row[:, :], NW).then_inc(init_done, 1)

            nc.vector.tensor_reduce(w_max[:, :], wk_raw.rearrange("p h m -> p (h m)"), mybir.AxisListType.X, ALU.max,
                                    apply_absolute_value=True).then_inc(w_max_in, 1)
            dve.wait_ge(w_max_mm, 1)
            nc.vector.tensor_reduce(w_pow[:, 0:1], ps[0:1, GN_BANK, 0:P], mybir.AxisListType.X, ALU.max)
            dve.drain()
            nc.vector.tensor_scalar(w_pow[:, 0:1], w_pow[:, 0:1], W_TINY, None, ALU.max)
            dve.drain()
            nc.vector.tensor_scalar(w_pow[:, 0:1].bitcast(I32), w_pow[:, 0:1].bitcast(I32), EXPONENT, None, ALU.bitwise_and)
            dve.drain()
            nc.vector.tensor_scalar(w_pow[:, 1:2], w_pow[:, 0:1], 1.0 / W_RANGE, None, ALU.mult)
            dve.drain()
            nc.vector.reciprocal(w_pow[:, 0:1], w_pow[:, 1:2]).then_inc(w_max_in, 1)
            dve.wait_ge(w_max_mm, 2)
            nc.vector.tensor_copy(wk_scale[:, :], ps[:, GN_BANK, 0:2])
            dve.drain()
            nc.vector.tensor_scalar(wk_raw, wk_raw, wk_scale[:, 0:1], None, ALU.mult)
            nc.vector.tensor_scalar(bk_row, bk_row, wk_scale[0:1, 0:1], None, ALU.mult)
            dve.drain()
            nc.vector.tensor_copy(wk_parts[:, 0, :, :], wk_raw)
            dve.drain()
            nc.vector.tensor_tensor(wk_parts[:, 1, :, :], wk_raw, wk_parts[:, 0, :, :], ALU.subtract)
            in_parts(k_parts, bk_row, CH)
            with dve.Fori(0, LOADS[1]) as j:
                stat_loaded(0, 2 * j, j, 0)
                stat_loaded(0, 2 * j + 1, j, 1)
            stat_loaded(0, NB - TAIL - 1, LOADS[0] - 1, 0)
            dve.wait_ge(x_placed, 16 * TAIL)
            for t in range(NB - TAIL, NB):
                stat(t)
            groupnorm_start()
            groupnorm_end(0)

            def image(i, last):
                def products(s, par, r):
                    row = BR * s + r
                    dve.wait_ge(w_ready, ROWS * i + row + 1)
                    if not (first(s, 1) and r < 2):
                        dve.wait_ge(sum_done, ROWS * i + row - 1)
                    nc.vector.tensor_copy(w_last[:, r % 2, :], ps[:, W_BANK + r % 2, NW - GROUPS:NW]).then_inc(w_last_ready, 1)
                    def multiply(lo, hi, slot):
                        kws = min(hi - lo, KW)
                        places = ring[:, slot:slot + (hi - lo + KW - 1) // KW, 0:kws, :]
                        return nc.vector.tensor_tensor(
                            prod[:, r % 2, lo:hi, :].rearrange("p k (g c) -> p (k g) c", c=GC),
                            ps[:, W_BANK + r % 2, GROUPS * lo:GROUPS * hi].unsqueeze(2).to_broadcast(
                                [P, GROUPS * (hi - lo), GC]),
                            places.rearrange("p r k (g c) -> p (r k g) c", c=GC), ALU.mult)

                    if first(s, 1) and r == 0:
                        dve.wait_ge(x_shifted[0][0], moves(i, 0, 0))
                    above = (BR * par + r - 1) % RING
                    if above == RING - 1:
                        multiply(0, KW, above)
                        multiply(KW, 2 * KW, 0).then_inc(mult_two, 1)
                    else:
                        multiply(0, 2 * KW, above).then_inc(mult_two, 1)
                    if r % 2 == 1 and not (isinstance(s, int) and s == NB - 1 and r == BR - 1):
                        nb, npar = (s, par) if r == 1 else (s + 1, 1 - par)
                        dve.wait_ge(x_shifted[npar][1 - r // 2], moves(i, nb, npar))
                    if not (first(s, 1) and r < 2):
                        dve.wait_ge(last_used, ROWS * i + row - 1)
                    multiply(2 * KW, TAPS - 1, (BR * par + r + 1) % RING).then_inc(mult_done, 1)

                def add_rows(s, pair):
                    q = 2 * s + pair
                    dve.wait_ge(inv_ready, ROWS * i + 2 * q + 2)
                    xa = X[:, :, bass.ds(q * 2 * COLS, 2 * COLS)]
                    nc.vector.tensor_tensor(xa, ps[:, INV_BANK + pair, :].rearrange("p (h n) -> p h n", h=2), xa,
                                            ALU.add).then_inc(x1_done, 1)

                def step(s, par):
                    if not ahead(s, 0):
                        return
                    products(s, par, 0)
                    products(s, par, 1)
                    if not first(s, 1):
                        add_rows(s - 1, 1)
                    products(s, par, 2)
                    if not first(s, 1):
                        dve.wait_ge(x1_done, PAIRS * i + 2 * s)
                        stat(s - 1)
                    if isinstance(s, int) and s == NB - 1:
                        nc.vector.memset(xt[:, 0:ROWT], 0.0)
                        dve.drain()
                    products(s, par, 3)
                    add_rows(s, 0)

                nc.vector.memset(ring[:, :, 0, :], 0.0)
                nc.vector.memset(ring[:, :, 2, :], 0.0).then_inc(ring_clear, 1)
                nc.vector.memset(ring[:, RING - 1, 1, :], 0.0)
                dve.drain()
                dve.wait_ge(x_placed, 16 * TAIL * (i + 1))
                block_steps(dve, step)
                add_rows(NB - 1, 1)
                dve.drain()
                stat(NB - 1)
                groupnorm_start()
                groupnorm_end(2 * i + 1)

                nc.vector.memset(xt_sb[:, :, :, CH:XO], 1.0)

                def split_x(u, par):
                    if not first(u, 2):
                        dve.wait_ge(kt_mm, PAIRS * i + u - 1)
                    for h in range(HALVES):
                        nc.vector.tensor_scalar(xs[:, par, h, :], X[:, h, bass.ds(u * 2 * COLS, 2 * COLS)],
                                                gn_rstd[:, h:h + 1], gn_shift[:, h:h + 1], ALU.mult, ALU.add)
                    dve.drain()
                    nc.vector.tensor_copy(x_parts[:, par, 0, :, :], xs[:, par, :, :])
                    dve.drain()
                    nc.vector.tensor_tensor(x_parts[:, par, 1, :, :], xs[:, par, :, :], x_parts[:, par, 0, :, :],
                                            ALU.subtract).then_inc(xs_ready, 1)

                def k_sum(u, par):
                    dve.wait_ge(kl_ready, PAIRS * i + u + 1)
                    if not first(u, 2):
                        dve.wait_ge(kx_done, PAIRS * i + u - 1)
                    k = k_sb[:, par, :, :].rearrange("p t m -> p (t m)")
                    nc.vector.tensor_scalar(k, ps[:, KZ_BANK + par, :], wk_scale[:, 1:2], 0.0, ALU.mult, ALU.max)
                    dve.drain()
                    nc.vector.tensor_tensor(k, k, k_act[:, par, :], ALU.add).then_inc(k_ready, 1)

                dve.drain()
                split_x(0, 0)
                split_x(1, 1)
                dve.wait_ge(w_loaded, 16 * (i + 1))
                for h in range(HALVES):
                    ins = nc.vector.tensor_scalar(wqv[:, h, 0:CH], wqv[:, h, 0:CH], gn_rstd[:, h:h + 1], None, ALU.mult)
                ins.then_inc(w_scaled, 1)
                k_sum(0, 0)
                dve.wait_ge(shift_mm, i + 1)
                nc.vector.tensor_tensor(q_bias[:, :], ps[:, SHIFT_BANK, 0:HALVES], bq_s[:, :], ALU.add).then_inc(bias_ready, 1)
                with dve.Fori(1, PAIRS // 2) as j:
                    split_x(2 * j, 0)
                    k_sum(2 * j - 1, 1)
                    split_x(2 * j + 1, 1)
                    k_sum(2 * j, 0)
                k_sum(PAIRS - 1, 1)

                dve.wait_ge(kx_done, PAIRS * (i + 1))
                for h in range(HALVES):
                    ins = nc.vector.tensor_copy(kx_sb[:, h, :], ps[:, KX_BANK + h, 0:XO])
                ins.then_inc(fold_in, 1)
                dve.drain()
                nc.vector.tensor_scalar(ksum_eps[:, :], kx_sb[:, :, CH], KSUM_EPS, None, ALU.add)
                dve.drain()
                for h in range(HALVES):
                    nc.vector.tensor_scalar(den_w[:, h, :], densel[:, h, :], ksum_eps[:, h:h + 1], None, ALU.mult)
                dve.wait_ge(fold_mm, 2 * i + 1)
                nc.vector.tensor_copy(ksum_row[:, :], ps[0:1, FOLD_BANK, 0:CH])
                nc.vector.tensor_copy(kxt_sb[:, :, :].rearrange("p h m -> p (h m)"), ps[:, FOLD_BANK + 1, :]).then_inc(fold_in, 1)
                dve.wait_ge(fold_mm, 2 * i + 2)
                for h in range(HALVES):
                    ins = nc.vector.tensor_tensor(kv_w[:, h, :], ps[:, FOLD_BANK, h * P:(h + 1) * P], headmask[:, :], ALU.mult)
                ins.then_inc(fold_in, 1)

                def q_relu(t, par):
                    for h in range(HALVES):
                        dve.wait_ge(qz_read, 2 * (NB * i + t) + h + 1)
                        nc.vector.tensor_scalar(q_sb[:, par, h, :], ps[:, QZ_BANK + 2 * par + h, :], q_bias[:, h:h + 1], 0.0,
                                                ALU.add, ALU.max).then_inc(q_relu_ready, 1)

                def reciprocals(t):
                    dve.wait_ge(den_mm, NB * i + t + 1)
                    nc.vector.reciprocal(rden, ps[:, DEN_BANK, 0:P])
                    dve.drain()
                    nc.vector.tensor_copy(rden_high, rden)
                    dve.drain()
                    nc.vector.scalar_tensor_tensor(rden_rest, rden_high, partsel[:, 0:1], rden, ALU.mult, ALU.add)
                    dve.drain()
                    nc.vector.tensor_copy(rden_high, rden_rest)
                    dve.drain()
                    nc.vector.scalar_tensor_tensor(rden_parts, rden_high, partsel[:, 1:2], rden_rest,
                                                   ALU.mult, ALU.add).then_inc(rden_ready, 1)

                def output(t):
                    dve.wait_ge(num_mm, NB * i + t + 1)
                    dve.wait_ge(wide_evac, 2 * (NB * i + t + 1))
                    if not first(t, 1):
                        dve.wait_ge(out_ready, NB * i + t)
                    nc.vector.tensor_tensor(ratio[:, :, :], ps[:, NUM_BANK:NUM_BANK + 2, :], rden_wide[:, :, :],
                                            ALU.mult).then_inc(num_read, 1)

                LAG = 4
                q_relu(0, 0)
                reciprocals(0)
                q_relu(1, 1)
                for t in range(1, LAG):
                    output(t - 1)
                    reciprocals(t)
                    q_relu(t + 1, (t + 1) % 2)
                    if not last:
                        dve.wait_ge(tail_loaded, 16 * TAIL * (i + 1))
                        for h in range(HALVES):
                            nc.vector.bn_stats(stats[:, h, NB - t, :], tail[:, TAIL - t, h, :])
                with dve.Fori(LAG // 2, NB // 2 - 1) as j:
                    for t, par in ((2 * j, 0), (2 * j + 1, 1)):
                        output(t - 1)
                        reciprocals(t)
                        q_relu(t + 1, 1 - par)
                        if not last:
                            stat_loaded(i + 1, t - LAG, j - LAG // 2, par)
                for t in (NB - 2, NB - 1):
                    output(t - 1)
                    reciprocals(t)
                    if t == NB - 2:
                        q_relu(NB - 1, 1)
                    if not last:
                        for b in ((NB - 6, NB - 5) if t == NB - 2 else (NB - 4,)):
                            stat_loaded(i + 1, b, b // 2, b % 2)
                if not last:
                    groupnorm_start()
                if last:
                    output(NB - 1)
                else:
                    groupnorm_end(2 * i + 2, lambda: output(NB - 1))
                    dve.wait_ge(out_ready, NB * (i + 1))

            images(dve, image)

        @block.tensor
        def _(pe):
            mm = nc.tensor.matmul

            def groupnorm(n):
                pe.wait_ge(gn_in, 3 * n + 1)
                mm(ps[:, GN_BANK, 0:4], gmean[:, :], mean_var[:, :, :].rearrange("p h s -> p (h s)"),
                   start=True, stop=True).then_inc(gn_mm, 1)
                pe.wait_ge(gn_in, 3 * n + 2)
                mm(ps[:, GN_BANK, 4:6], gmean[:, :], gn_dev[:, :], start=True, stop=True).then_inc(gn_mm, 1)

            pe.wait_ge(init_done, 1)
            pe.wait_ge(w_max_in, 1)
            mm(ps[0:1, GN_BANK, 0:P], w_max[:, :], ident[:, :], start=True, stop=True).then_inc(w_max_mm, 1)
            pe.wait_ge(w_max_in, 2)
            mm(ps[:, GN_BANK, 0:2], one_row, w_pow[:, :], start=True, stop=True).then_inc(w_max_mm, 1)
            groupnorm(0)

            def image(i, last):
                def y_of(b, par):
                    pe.wait_ge(xn_ready, NB * i + b + 1)
                    if not first(b, 1):
                        pe.wait_ge(y_evac, NB * i + b)
                    for h in range(HALVES):
                        ins = mm(ps[:, Y_BANK, :], w1_s[:, h, :],
                                 xn[:, par, h, :], start=(h == 0), stop=(h == HALVES - 1))
                    ins.then_inc(y_mm, 1)

                def fill(b, par, f):
                    if not first(b, 1):
                        pe.wait_ge(xt_evac, FILLS * (NB * i + b) + f - 1)
                    for c in range(4):
                        r, h = 2 * f + c // 2, c % 2
                        ins = mm(ps[:, XT_BANK + f, c * P:(c + 1) * P], xn[:, par, h, r * COLS:(r + 1) * COLS], ident[:, :],
                                 start=True, stop=True, is_transpose=True)
                    ins.then_inc(xt_mm, 1)

                def depthwise(b, par):
                    pe.wait_ge(y_halo, NB * i + b + 1)
                    if not first(b, 1):
                        pe.wait_ge(y2_evac, NB * i + b)
                    for k in range(TAPS):
                        kh, kw = divmod(k, KW)
                        ins = mm(ps[:, Y2_BANK, 0:2 * COLS].rearrange("p (r c) -> p r c", r=2), wdiag[:, k, :],
                                 y[:, par, kh:kh + 2, kw:kw + COLS], start=(k == 0), stop=(k == TAPS - 1))
                    ins.then_inc(y2_mm, 1)

                def weights(s, par, r):
                    row = BR * s + r
                    if r == 0:
                        pe.wait_ge(y2_evac, NB * i + s + 1)
                    if not (first(s, 1) and r < 2):
                        pe.wait_ge(mult_done, ROWS * i + row - 1)
                    lo = CR * (r // 2)
                    mm(ps[:, W_BANK + r % 2, 0:NW], ones_bf[:, 0:P], b2_parts[:, :], start=True, stop=False)
                    mm(ps[:, W_BANK + r % 2, 0:NW], y2[lo:lo + CR, par, r % 2, :], w2_s[lo:lo + CR, :],
                       start=False, stop=True).then_inc(w_ready, 1)

                def gather_last(s, par, r):
                    pe.wait_ge(last_made, ROWS * i + BR * s + r + 1)
                    if not first(s, 1) and r % 2 == 0:
                        pe.wait_ge(x1_done, PAIRS * i + 2 * s + r // 2 - 1)
                    pe.wait_ge(mult_done, ROWS * i + BR * s + r + 1)
                    for h in range(HALVES):
                        o = h * 256 + (r % 2) * P
                        for k in (TAPS - 2, TAPS - 1):
                            ins = mm(ps[:, INV_BANK + r // 2, o:o + P], prod[:, r % 2, k, h * P:(h + 1) * P], ident[:, :],
                                     start=(r % 2 == 0 and h == 0 and k == TAPS - 2), stop=False, is_transpose=True)
                    ins.then_inc(last_used, 1)

                def gather(s, par, r):
                    pe.wait_ge(sum_done, ROWS * i + BR * s + r + 1)
                    for h in range(HALVES):
                        o = h * 256 + (r % 2) * P
                        for k in range(KW):
                            ins = mm(ps[:, INV_BANK + r // 2, o:o + P], sums[:, r % 2, k, h * P:(h + 1) * P], ident[:, :],
                                     start=False, stop=(r % 2 == 1 and h == 1 and k == KW - 1), is_transpose=True)
                    ins.then_inc(inv_ready, 1)

                def step(s, par):
                    now, before, nxt, nxt2 = ahead(s, 0), ahead(s, -1), ahead(s, 1), ahead(s, 2)
                    if not now:
                        y_of(s + 2, par)
                        if s == -2:
                            for f in range(FILLS):
                                fill(0, 0, f)
                        else:
                            depthwise(0, 0)
                        return
                    weights(s, par, 0)
                    if before:
                        gather_last(s - 1, 1 - par, 2)
                        gather(s - 1, 1 - par, 2)
                    if nxt2:
                        y_of(s + 2, par)
                    weights(s, par, 1)
                    if nxt:
                        fill(s + 1, 1 - par, 0)
                    if before:
                        gather_last(s - 1, 1 - par, 3)
                        gather(s - 1, 1 - par, 3)
                    weights(s, par, 2)
                    if nxt:
                        fill(s + 1, 1 - par, 1)
                    gather_last(s, par, 0)
                    gather(s, par, 0)
                    weights(s, par, 3)
                    if nxt:
                        depthwise(s + 1, 1 - par)
                    gather_last(s, par, 1)
                    gather(s, par, 1)

                block_steps(pe, step)
                for r in (2, 3):
                    gather_last(NB - 1, 1, r)
                    gather(NB - 1, 1, r)
                groupnorm(2 * i + 1)

                def k_of(u, par):
                    pe.wait_ge(xs_ready, PAIRS * i + u + 1)
                    if not first(u, 2):
                        pe.wait_ge(k_ready, PAIRS * i + u - 1)
                    for t in range(2):
                        z = ps[:, KZ_BANK + par, t * CH:(t + 1) * CH]
                        mm(z, ones_bf[:, 0:P], k_parts[:, :], start=True, stop=False)
                        for h in range(HALVES):
                            for xp, wp in ((0, 0), (0, 1), (1, 0)):
                                ins = mm(z, x_parts[:, par, xp, h, t * P:(t + 1) * P], wk_parts[:, wp, h, :],
                                         start=False, stop=(h == 1 and xp == 1))
                    ins.then_inc(kz_mm, 1)
                    if not first(u, 2):
                        pe.wait_ge(kt_evac, PAIRS * i + u - 1)
                    for t in range(2):
                        for h in range(HALVES):
                            o = t * CH + h * P
                            ins = mm(ps[:, KT_BANK + par, o:o + P], xs[:, par, h, t * P:(t + 1) * P], ident[:, :],
                                     start=True, stop=True, is_transpose=True)
                    ins.then_inc(kt_mm, 1)

                def kx_add(u, par):
                    pe.wait_ge(k_ready, PAIRS * i + u + 1)
                    pe.wait_ge(kt_evac, PAIRS * i + u + 1)
                    for t in range(2):
                        for h in range(HALVES):
                            ins = mm(ps[:, KX_BANK + h, 0:XO], k_sb[:, par, t, h * P:(h + 1) * P], xt_sb[:, par, t, :],
                                     start=(first(u, 1) and t == 0), stop=(isinstance(u, int) and u == PAIRS - 1 and t == 1))
                    ins.then_inc(kx_done, 1)

                k_of(0, 0)
                k_of(1, 1)
                pe.wait_ge(w_scaled, i + 1)
                for h in range(HALVES):
                    for ih in range(HALVES):
                        ins = mm(ps[:, SHIFT_BANK, h:h + 1], wqv[:, ih, h * P:(h + 1) * P], gn_neg[:, ih:ih + 1],
                                 start=(ih == 0), stop=(ih == HALVES - 1))
                ins.then_inc(shift_mm, 1)
                kx_add(0, 0)
                with pe.Fori(1, PAIRS // 2) as j:
                    k_of(2 * j, 0)
                    kx_add(2 * j - 1, 1)
                    k_of(2 * j + 1, 1)
                    kx_add(2 * j, 0)
                kx_add(PAIRS - 1, 1)

                def q_of(t, par, h):
                    if not first(t, 2):
                        pe.wait_ge(q_ready, 2 * (NB * i + t) + h - 3)
                    z = ps[:, QZ_BANK + 2 * par + h, :]
                    for ih in range(HALVES):
                        ins = mm(z, wqv[:, ih, h * P:(h + 1) * P], X[:, ih, bass.ds(t * BP, BP)], start=(ih == 0), stop=(ih == 1))
                    ins.then_inc(qz_mm, 1)

                q_of(0, 0, 0)
                pe.wait_ge(fold_in, 3 * i + 1)
                for h in range(HALVES):
                    mm(ps[0:1, FOLD_BANK, h * P:(h + 1) * P], kx_sb[:, h, CH:XO], ident[:, :], start=True, stop=True)
                for ih in range(HALVES):
                    for h in range(HALVES):
                        o = ih * CH + h * P
                        ins = mm(ps[:, FOLD_BANK + 1, o:o + P], kx_sb[:, h, ih * P:(ih + 1) * P], ident[:, :],
                                 start=True, stop=True, is_transpose=True)
                ins.then_inc(fold_mm, 1)
                q_of(0, 0, 1)
                pe.wait_ge(fold_in, 3 * i + 2)
                for h in range(HALVES):
                    kv = ps[:, FOLD_BANK, h * P:(h + 1) * P]
                    for ih in range(HALVES):
                        mm(kv, kxt_sb[:, ih, h * P:(h + 1) * P], wqv[:, ih, CH + h * P:CH + (h + 1) * P],
                           start=(ih == 0), stop=False)
                    ins = mm(kv, ksum_row[:, h * P:(h + 1) * P], bv_row[:, h * P:(h + 1) * P],
                             start=False, stop=True)
                ins.then_inc(fold_mm, 1)

                pe.wait_ge(fold_in, 3 * i + 3)

                def denominators(t, par):
                    pe.wait_ge(q_ready, 2 * (NB * i + t) + 2)
                    if not first(t, 1):
                        pe.wait_ge(wide_evac, 2 * (NB * i + t))
                    for h in range(HALVES):
                        for c in range(BR):
                            ins = mm(ps[32 * c:32 * c + DEN_COLS, DEN_BANK, 0:P], den_w[:, h, :],
                                     q_sb[:, par, h, c * P:(c + 1) * P], start=(h == 0), stop=(h == 1),
                                     tile_position=(0, 32 * c))
                    ins.then_inc(den_mm, 1)

                def numerators(t, par):
                    if not first(t, 1):
                        pe.wait_ge(num_read, NB * i + t)
                    for h in range(HALVES):
                        ins = mm(ps[:, NUM_BANK + h, :], kv_w[:, h, :], q_sb[:, par, h, :], start=True, stop=True)
                    ins.then_inc(num_mm, 1)

                def widen(t):
                    pe.wait_ge(rden_ready, NB * i + t + 1)
                    for h in range(HALVES):
                        for c in range(BR):
                            ins = mm(ps[:, WIDE_BANK[h], c * P:(c + 1) * P], headsel[:, c, h, :], rden_parts[:, :],
                                     start=True, stop=True)
                        ins.then_inc(wide_mm, 1)

                def c_step(t, par, more):
                    if more:
                        q_of(t + 1, 1 - par, 0)
                    denominators(t, par)
                    if more:
                        q_of(t + 1, 1 - par, 1)
                    numerators(t, par)
                    widen(t)

                pe.wait_ge(sel_loaded, 16 * (i + 1))
                c_step(0, 0, True)
                c_step(1, 1, True)
                with pe.Fori(1, NB // 2 - 1) as j:
                    c_step(2 * j, 0, True)
                    c_step(2 * j + 1, 1, True)
                c_step(NB - 2, 0, True)
                c_step(NB - 1, 1, False)
                if not last:
                    groupnorm(2 * i + 2)
                    pe.wait_ge(num_read, NB * (i + 1))

            images(pe, image)


_OUT = "out_dram"


def kernel(**inputs):
    import numpy as np
    import concourse.bacc as bacc
    from concourse.bass_utils import run_bass_kernel_spmd

    a = {k: np.asarray(v) for k, v in inputs.items()}
    w1t = a["L0_conv_w1"].T
    w2t = a["L0_conv_w2"].reshape(GROUPS, TAPS, CR).transpose(2, 1, 0).reshape(CR, NW)
    arrays = {
        "x": a["x"],
        "w1t": np.concatenate([w1t, w1t], axis=1),
        "b1": np.concatenate([a["L0_conv_b1"]] * 2).reshape(P, 1),
        "wd": np.concatenate([a["L0_conv_wd"].reshape(CR, TAPS)] * 2),
        "bd": np.concatenate([a["L0_conv_bd"]] * 2).reshape(P, 1),
        "w2t": np.concatenate([w2t, w2t]),
        "b2": a["L0_conv_b2"].reshape(GROUPS, TAPS).T.reshape(1, NW),
        "wk": a["L1_conv_Wk"].T,
        "bk": a["L1_conv_bk"].reshape(1, CH),
        "wqv": np.concatenate([a["L1_conv_Wq"].T, a["L1_conv_Wv"].T], axis=1),
        "bq": a["L1_conv_bq"].reshape(HALVES, P).T,
        "bv": a["L1_conv_bv"].reshape(1, CH),
    }
    c = np.arange(P)
    head = c[:, None] // 32 + 4 * np.arange(HALVES)[None, :]
    sel = (head[:, :, None] == (np.arange(DEN_COLS) % HEADS)[None, None, :]).astype(np.float32)
    once = (sel * (np.arange(DEN_COLS) < PARTS * HEADS)).transpose(2, 1, 0)[:, None]
    part = (c % DEN_COLS) // HEADS
    arrays.update({
        "ident": np.eye(P, dtype=np.float32),
        "gmean": ((c[:, None] // 8 == c[None, :] // 8) / 8.0).astype(np.float32),
        "headmask": (c[:, None] // 32 == c[None, :] // 32).astype(np.float32),
        "densel": sel,
        "partsel": -(part[:, None] > np.arange(PARTS - 1)[None, :]).astype(np.float32),
        "headsel": np.concatenate([once * (np.arange(BR) == q)[None, :, None, None] for q in range(BR)]).astype(mybir.dt.np(BF16)),
    })
    arrays = {f"{k}_in": np.ascontiguousarray(v) for k, v in arrays.items()}
    nc = bacc.Bacc("TRN2", target_bir_lowering=False, num_devices=1)
    args = [nc.dram_tensor(k, v.shape, mybir.dt.from_np(v.dtype), kind="ExternalInput").ap() for k, v in arrays.items()]
    args.append(nc.dram_tensor(_OUT, (IMAGES, CH, ROWS, COLS), F32, kind="ExternalOutput").ap())
    two_block_kernel(nc, *args)
    r = run_bass_kernel_spmd(nc, [arrays], core_ids=[0])
    return r.results[0][_OUT]
```
